# Optimizing a Trainium2 kernel written in Bass

```python
import numpy as np
import jax
import jax.numpy as jnp

def _softmax(x, axis=-1):
    return jax.nn.softmax(x, axis=axis)

def _gelu(x):
    return jax.nn.gelu(x, approximate=True)

def _silu(x):
    return jax.nn.silu(x)

def _sigmoid(x):
    return jax.nn.sigmoid(x)

def _layernorm(x, axis=-1, eps=1e-05):
    m = jnp.mean(x, axis=axis, keepdims=True)
    v = jnp.var(x, axis=axis, keepdims=True)
    return (x - m) / jnp.sqrt(v + eps)

def _scatter_add(tgt, idx, src, axis=0):
    return tgt.at[idx].add(src)

def _segment_sum(src, seg, n):
    return jax.ops.segment_sum(src, seg, n)
kernel_name = 'mk_cond_resid_d2_seqx_r4_5b225a'

def setup_inputs(seed: int=0):
    np.random.seed(seed)
    _w = jnp.asarray

    def _rec_inputs():
        import jax
        import jax.numpy as jnp
        _rk = jax.random.key(seed)
        x = -0.0002928 + 1 * jax.random.normal(jax.random.fold_in(_rk, 1), (2, 1024, 256), jnp.float32)
        _lenS = 1024 - jax.random.randint(jax.random.fold_in(_rk, 7), (2,), 0, max(1, 1024 // 4) + 1, jnp.int32)
        _lenS2 = 1024 - jax.random.randint(jax.random.fold_in(_rk, 8), (2,), 0, max(1, 1024 // 4) + 1, jnp.int32)
        cond_1024 = -0.00356592 + 0.997978 * jax.random.normal(jax.random.fold_in(_rk, 11), (2, 256), jnp.float32)
        return (x, cond_1024)
    x, cond_1024 = _rec_inputs()

    def _L0_cond_setup():
        import jax, jax.numpy as jnp
        import numpy as np
        B, T, D = (128, 32, 256)
        ADA, INTER, RANK = (256, 256, 8)
        LN_EPS = 1e-05

        def _layernorm(x, g, b):
            mu = jnp.mean(x, axis=-1, keepdims=True)
            var = jnp.var(x, axis=-1, keepdims=True)
            return (x - mu) * jax.lax.rsqrt(var + LN_EPS) * g + b
        key = jax.random.key(seed)
        ks = jax.random.split(key, 9)
        return {'x': jax.random.normal(ks[0], (B, T, D), dtype=jnp.float32), 'ada_emb': jax.random.normal(ks[1], (B, ADA), dtype=jnp.float32), 'base_layer': jax.random.normal(ks[2], (D, D), dtype=jnp.float32), 'w1': jax.random.normal(ks[3], (ADA, INTER), dtype=jnp.float32) * 0.02, 'b1': jnp.zeros((INTER,), dtype=jnp.float32), 'w2': jax.random.normal(ks[4], (INTER, 2 * D * RANK), dtype=jnp.float32) * 0.02, 'b2': jnp.zeros((2 * D * RANK,), dtype=jnp.float32), 'ln_g': jnp.ones((ADA,), dtype=jnp.float32), 'ln_b': jnp.zeros((ADA,), dtype=jnp.float32)}
    _L0_cond_all = _L0_cond_setup()
    _L0_cond_in = {k: v for k, v in _L0_cond_all.items() if k in ('base_layer', 'w1', 'b1', 'w2', 'b2', 'ln_g', 'ln_b')}
    del _L0_cond_all

    def _L1_cond_setup():
        import jax, jax.numpy as jnp
        import numpy as np
        N, T, D, H = (64, 128, 256, 256)
        key = jax.random.key(seed)
        k1, k2, k3, k4 = jax.random.split(key, 4)
        x = jax.random.normal(k1, (N, T, D), dtype=jnp.float32)
        h0 = jax.random.normal(k2, (N, H), dtype=jnp.float32)
        Wx = jax.random.normal(k3, (D, H), dtype=jnp.float32) / np.sqrt(D)
        Wh = jax.random.normal(k4, (H, H), dtype=jnp.float32) / np.sqrt(H)
        b = jnp.zeros((H,), dtype=jnp.float32)
        return {'x': x, 'h0': h0, 'Wx': Wx, 'Wh': Wh, 'b': b}
    _L1_cond_all = _L1_cond_setup()
    _L1_cond_in = {k: v for k, v in _L1_cond_all.items() if k in ('Wx', 'Wh', 'b')}
    del _L1_cond_all
    return {'x': x, 'cond_1024': cond_1024, 'L0_cond_base_layer': _L0_cond_in['base_layer'], 'L0_cond_w1': _L0_cond_in['w1'], 'L0_cond_b1': _L0_cond_in['b1'], 'L0_cond_w2': _L0_cond_in['w2'], 'L0_cond_b2': _L0_cond_in['b2'], 'L0_cond_ln_g': _L0_cond_in['ln_g'], 'L0_cond_ln_b': _L0_cond_in['ln_b'], 'L1_cond_Wx': _L1_cond_in['Wx'], 'L1_cond_Wh': _L1_cond_in['Wh'], 'L1_cond_b': _L1_cond_in['b']}

def reference(x, cond_1024, L0_cond_base_layer, L0_cond_w1, L0_cond_b1, L0_cond_w2, L0_cond_b2, L0_cond_ln_g, L0_cond_ln_b, L1_cond_Wx, L1_cond_Wh, L1_cond_b):
    import jax
    import jax.numpy as jnp

    def _L0_cond_ref(x, ada_emb, base_layer, w1, b1, w2, b2, ln_g, ln_b):
        import jax, jax.numpy as jnp
        import numpy as np
        B, T, D = (128, 32, 256)
        ADA, INTER, RANK = (256, 256, 8)
        LN_EPS = 1e-05

        def _layernorm(x, g, b):
            mu = jnp.mean(x, axis=-1, keepdims=True)
            var = jnp.var(x, axis=-1, keepdims=True)
            return (x - mu) * jax.lax.rsqrt(var + LN_EPS) * g + b
        b, t, d = x.shape
        ae = _layernorm(ada_emb, ln_g, ln_b)
        h = jax.nn.gelu(ae @ w1 + b1, approximate=False)
        xw = h @ w2 + b2
        x_a, x_b = jnp.split(xw, 2, axis=-1)
        x_a = x_a.reshape(b, d, RANK)
        x_b = x_b.reshape(b, d, RANK)
        layer = base_layer[None, :, :] + jnp.einsum('bdr,bkr->bdk', x_a, x_b)
        out = jnp.einsum('btc,bco->bto', x, layer)
        return x + out

    def _L1_cond_ref(x, h0, Wx, Wh, b):
        import jax, jax.numpy as jnp
        import numpy as np
        N, T, D, H = (64, 128, 256, 256)
        xW = jnp.einsum('ntd,dh->nth', x, Wx) + b
        xW_t = jnp.swapaxes(xW, 0, 1)

        def step(prev_h, xw):
            next_h = jnp.tanh(prev_h @ Wh + xw)
            return (next_h, next_h)
        _, h_t = jax.lax.scan(step, h0, xW_t)
        return jnp.swapaxes(h_t, 0, 1)
    x = x + _L0_cond_ref(x, cond_1024, L0_cond_base_layer, L0_cond_w1, L0_cond_b1, L0_cond_w2, L0_cond_b2, L0_cond_ln_g, L0_cond_ln_b)
    x = x + _L1_cond_ref(x, cond_1024, L1_cond_Wx, L1_cond_Wh, L1_cond_b)
    return x

_drawn_inputs = setup_inputs


def setup_inputs(seed=0):
    import zlib

    import numpy as np

    out = dict(_drawn_inputs(seed))
    spreads = {'L0_cond_b1': (0.0, 0.8),
     'L0_cond_b2': (0.0, 0.1),
     'L0_cond_ln_g': (1.0, 0.6),
     'L0_cond_ln_b': (0.0, 0.8),
     'L1_cond_b': (0.0, 0.8)}
    factors = {'L1_cond_Wh': 5.885}
    for name, (base, spread) in spreads.items():
        noise = np.random.default_rng([zlib.crc32(name.encode()), seed]).standard_normal(out[name].shape)
        drawn = base * np.exp(spread * noise) if base else spread * noise
        out[name] = jnp.asarray(drawn.astype(out[name].dtype))
    for name, factor in factors.items():
        out[name] = (out[name] * factor).astype(out[name].dtype)
    return out
```

```python
from contextlib import ExitStack

import numpy as np
import concourse.bass as bass
from concourse import mybir

F32, F16 = mybir.dt.float32, mybir.dt.float16
ACT, ALU = mybir.ActivationFunctionType, mybir.AluOpType

P = 128
NB = 2
T = 1024
D = 256
NM = D // P
RANK = 8
COLS = NM * NB
BLOCK = 32
HALF = BLOCK // 2
NBLOCK = T // BLOCK
PAIRS = HALF // 2
SCALE = 256.0
LN_EPS = 1e-5
A, B = 0, 1


def cond_recurrence(nc, x, cond, base, w1, b1, w2, b2, ln_g, ln_b, wx, wh, b, out):
    ctx = ExitStack()
    with ctx:
        def sb(name, shape, dt=F32):
            return ctx.enter_context(nc.sbuf_tensor(name, shape, dt))

        def pb(name, shape, dt=F32):
            return ctx.enter_context(nc.psum_tensor(name, shape, dt))

        def sem(name):
            return ctx.enter_context(nc.semaphore(name))

        ident = sb("ident", [P, P])
        ident16 = sb("ident16", [P, P], F16)
        wh_f = sb("wh_f", [P, NM, D])
        wx_f = sb("wx_f", [P, NM, D])
        base_f = sb("base_f", [P, NM, D])
        w1_f = sb("w1_f", [P, NM, D])
        w2_f = sb("w2_f", [P, NM, 2 * D * RANK])
        wh_s = sb("wh_s", [P, 2, NM, D], F16)
        wx_s = sb("wx_s", [P, 2, NM, D], F16)
        lay_f = sb("lay_f", [P, NB, NM, D])
        lay_s = sb("lay_s", [P, 2, NB, NM, D], F16)
        b_row = sb("b_row", [1, D])
        b_rest = sb("b_rest", [1, D])
        b_parts = sb("b_parts", [1, 3, D], F16)
        b_w = sb("b_w", [3, D], F16)
        ones = sb("ones", [3, PAIRS * NB], F16)
        cond_r = sb("cond_r", [NB, D])
        cond_n = sb("cond_n", [NB, D])
        cond_c = sb("cond_c", [P, COLS])
        stats = sb("stats", [NB, 6])
        mv = sb("mv", [NB, 2])
        veps = sb("veps", [NB, 1])
        rstd = sb("rstd", [NB, 2])
        vec_r = sb("vec_r", [3 * NM, P])
        vec_c = sb("vec_c", [P, 3, NM])
        ae = sb("ae", [P, NM, NB])
        hid = sb("hid", [P, NM, NB])
        ab_row = sb("ab_row", [NB, 2 * D * RANK])
        b2_c = sb("b2_c", [P, 4, RANK])
        ab_f = sb("ab_f", [P, 4, NB, RANK])
        ab_st = sb("ab_st", [P, 4, NB, 4, RANK], F16)
        ab_t = sb("ab_t", [NB * 4 * RANK, 4, P], F16)
        x_in = sb("x_in", [P, P])
        x_f = sb("x_f", [P, BLOCK, NM, NB])
        x_s = sb("x_s", [P, 2, BLOCK, NM, NB], F16)
        y_new = sb("y_new", [P, BLOCK, NM, NB])
        y_cur = sb("y_cur", [P, BLOCK, NM, NB])
        y_s = sb("y_s", [P, 2, BLOCK, NM, NB], F16)
        h_f = sb("h_f", [P, BLOCK, COLS])
        h_hi = sb("h_hi", [P, 2, NM, NB], F16)
        h_lo = sb("h_lo", [P, 2, NM, NB], F16)
        o_sum = sb("o_sum", [P, HALF * COLS])
        o_row = sb("o_row", [HALF * COLS, P])

        acc = [[pb(f"acc{half}{par}", [P, 512]) for par in range(2)] for half in range(2)]
        p_x = pb("p_x", [P, 512])
        p_y = pb("p_y", [P, 512])
        p_o = pb("p_o", [P, 512])
        p_ab = pb("p_ab", [P, 4 * P], F16)

        s_cond, s_vec, s_w1, s_b2, s_base = sem("s_cond"), sem("s_vec"), sem("s_w1"), sem("s_b2"), sem("s_base")
        s_w2 = [sem(f"s_w2_{q}") for q in range(4)]
        s_wh, s_wx, s_b, s_bw = sem("s_wh"), sem("s_wx"), sem("s_b"), sem("s_bw")
        s_ident = sem("s_ident")
        s_ones = sem("s_ones")
        s_hi = sem("s_hi")
        s_split = sem("s_split")
        s_bparts = sem("s_bparts")
        s_var = sem("s_var")
        s_sqrt = sem("s_sqrt")
        s_norm = sem("s_norm")
        s_turn0 = sem("s_turn0")
        s_condc = sem("s_condc")
        s_vecc = sem("s_vecc")
        s_ae = sem("s_ae")
        s_hmm = sem("s_hmm")
        s_hid = sem("s_hid")
        s_abmm = sem("s_abmm")
        s_abrow = sem("s_abrow")
        s_abcol = sem("s_abcol")
        s_abst = sem("s_abst")
        s_abt = sem("s_abt")
        s_abts = sem("s_abts")
        s_lmm = sem("s_lmm")
        s_lay = sem("s_lay")
        s_layhi = sem("s_layhi")
        s_layer = sem("s_layer")
        s_link = sem("s_link")
        s_sum = [sem("s_sumA"), sem("s_sumB")]
        s_hhi = [sem("s_hhiA"), sem("s_hhiB")]
        s_hf = [sem("s_hfA"), sem("s_hfB")]
        s_hlo = [sem("s_hloA"), sem("s_hloB")]
        s_xload = sem("s_xload")
        s_xfree = sem("s_xfree")
        s_xturn = sem("s_xturn")
        s_xsplit = sem("s_xsplit")
        s_ymm = sem("s_ymm")
        s_ysplit = sem("s_ysplit")
        s_osum = sem("s_osum")
        s_oturn = sem("s_oturn")
        s_orow = sem("s_orow")
        s_store = sem("s_store")
        s_ofree = sem("s_ofree")
        s_own = sem("s_own")

        x_rows = x.rearrange("b t (m p) -> t m b p", p=P)
        out_rows = out.rearrange("b t (m p) -> t m b p", p=P)
        cols = lambda ap: ap.rearrange("p t m b -> p (t m b)")

        def take(eng, s, n):
            eng.wait_ge(s, n)
            eng.sem_clear(s)

        def turn_x():
            take(nc.tensor, s_xload, 16)
            nc.tensor.transpose(p_x[:, 0:P], x_in[:, :], ident[:, :]).then_inc(s_xturn, 1)

        PARTS = [(0, 0), (1, 0), (0, 1), (1, 1)]

        def layer_products():
            first = True
            todo = [(bb, mo, ki, pw, px) for bb in range(NB) for mo in range(NM)
                    for ki in range(NM) for pw, px in PARTS]
            py = p_y[:, 0:P].rearrange("p (t m b) -> p t m b", m=NM, b=NB)
            for bb, mo, ki, pw, px in todo:
                yield nc.tensor.matmul(py[:, :, mo, bb], lay_s[:, pw, bb, ki, mo * P:(mo + 1) * P],
                                       x_s[:, px, :, ki, bb], start=first, stop=True, skip_group_check=True)
                first = False

        def input_products(half):
            for par in range(2):
                av = acc[half][par][:, 0:PAIRS * COLS].rearrange("p (t m b) -> p t m b", m=NM, b=NB)
                for mo in range(NM):
                    yield nc.tensor.matmul(av[:, :, mo, :], b_w[:, mo * P:(mo + 1) * P], ones[:, :],
                                           start=mo == 0, stop=True, skip_group_check=True)
                for mo in range(NM):
                    for ki in range(NM):
                        for pw, py in PARTS:
                            t0 = half * HALF + par
                            yield nc.tensor.matmul(
                                av[:, :, mo, :], wx_s[:, pw, ki, mo * P:(mo + 1) * P],
                                y_s[:, py, t0:t0 + HALF - 1:2, ki, :],
                                start=False, stop=True, skip_group_check=True)

        def some(products, n):
            last = None
            for _ in range(n):
                nxt = next(products, None)
                last = nxt if nxt is not None else last
            return last

        def turn_out():
            take(nc.tensor, s_osum, 1)
            nc.tensor.transpose(p_o[0:HALF * COLS, 0:P], o_sum[:, :], ident[:, :]).then_inc(s_oturn, 1)

        def split_x_high():
            take(nc.vector, s_xturn, 1)
            nc.vector.tensor_copy(cols(x_f[:, :, :, :]), p_x[:, 0:P]).then_inc(s_xfree, 1)
            nc.vector.tensor_copy(cols(x_s[:, 0]), p_x[:, 0:P]).then_inc(s_own, 1)

        def split_x_low(own):
            nc.vector.wait_ge(s_own, own)
            nc.vector.tensor_sub(cols(x_s[:, 1]), p_x[:, 0:P], cols(x_s[:, 0])).then_inc(s_xsplit, 1)

        def finish_y(own):
            take(nc.vector, s_ymm, 1)
            nc.vector.scalar_tensor_tensor(cols(y_new[:, :, :, :]), cols(x_f[:, :, :, :]), 2.0, p_y[:, 0:P],
                                           ALU.mult, ALU.add).then_inc(s_own, 1)

        def split_y_high(own):
            nc.vector.wait_ge(s_own, own)
            nc.vector.tensor_copy(cols(y_s[:, 0]), cols(y_new[:, :, :, :])).then_inc(s_own, 1)

        def split_y_low(own):
            nc.vector.wait_ge(s_own, own)
            nc.vector.tensor_sub(cols(y_s[:, 1]), cols(y_new[:, :, :, :]), cols(y_s[:, 0])).then_inc(s_ysplit, 1)

        def sum_out(half):
            sl = slice(half * HALF, (half + 1) * HALF)
            nc.vector.tensor_add(o_sum[:, :], cols(y_cur[:, sl]),
                                 h_f[:, sl, :].rearrange("p t c -> p (t c)")).then_inc(s_osum, 1)

        def row_out():
            take(nc.vector, s_oturn, 1)
            take(nc.vector, s_ofree, 1)
            nc.vector.tensor_copy(o_row[:, :], p_o[0:HALF * COLS, 0:P]).then_inc(s_orow, 1)

        def tensor_half(half, pieces):
            for u in range(HALF):
                par = u % 2
                dst = acc[half][par][:, (u // 2) * COLS:(u // 2 + 1) * COLS]
                nc.tensor.wait_ge(s_hhi[half], u + 1)
                for pw in range(2):
                    for mo in range(NM):
                        for ki in range(NM):
                            nc.tensor.matmul(dst[:, mo * NB:(mo + 1) * NB], wh_s[:, pw, ki, mo * P:(mo + 1) * P],
                                             h_hi[:, par, ki, :], start=False, stop=True, skip_group_check=True)
                nc.tensor.wait_ge(s_hlo[half], u + 1)
                for mo in range(NM):
                    for ki in range(NM):
                        last = nc.tensor.matmul(dst[:, mo * NB:(mo + 1) * NB], wh_s[:, 0, ki, mo * P:(mo + 1) * P],
                                                h_lo[:, par, ki, :], start=False, stop=True, skip_group_check=True)
                last.then_inc(s_sum[half], 1)
                if u in pieces:
                    pieces[u]()
            nc.tensor.sem_clear(s_hhi[half])
            nc.tensor.sem_clear(s_hlo[half])

        def give_h(n, src, func, scale, final=False):
            half, par, slot = (n // HALF) % 2, n % 2, (n - 1) % BLOCK
            if not final:
                nc.scalar.activation(h_hi[:, par].rearrange("p m b -> p (m b)"), src, func,
                                     scale=scale).then_inc(s_hhi[half], 1)
            nc.scalar.activation(h_f[:, slot, :], src, func, scale=scale).then_inc(s_hf[half], 1)

        def scalar_half(half, final=False):
            for u in range(HALF):
                nc.scalar.wait_ge(s_sum[half], u + 1)
                give_h(half * HALF + u + 1, acc[half][u % 2][:, (u // 2) * COLS:(u // 2 + 1) * COLS],
                       ACT.Tanh, 1.0 / SCALE, final=final and u == HALF - 1)
            nc.scalar.sem_clear(s_sum[half])

        def vector_half(half, pieces):
            for u in range(HALF):
                par, slot = u % 2, (half * HALF + u - 1) % BLOCK
                nc.vector.wait_ge(s_hf[half], u + 1)
                nc.vector.tensor_sub(h_lo[:, par].rearrange("p m b -> p (m b)"), h_f[:, slot, :],
                                     h_hi[:, par].rearrange("p m b -> p (m b)")).then_inc(s_hlo[half], 1)
                if u in pieces:
                    pieces[u]()
            nc.vector.sem_clear(s_hf[half])

        def tensor_B(more):
            ps, xs = layer_products(), input_products(A)
            pieces = {1: turn_out}
            if more:
                def turn():
                    turn_x()
                def y_part(n, wait, end):
                    def piece():
                        if wait:
                            take(nc.tensor, s_xsplit, 1)
                        last = some(ps, n)
                        if end:
                            last.then_inc(s_ymm, 1)
                    return piece
                def acc_part(n, wait):
                    def piece():
                        if wait:
                            take(nc.tensor, s_ysplit, 1)
                        some(xs, n)
                    return piece
                pieces[0] = turn
                for k in range(4):
                    pieces[4 + k] = y_part(8, k == 0, k == 3)
                for k in range(4):
                    pieces[12 + k] = acc_part(9, k == 0)
            return pieces

        def vector_B(more):
            pieces = {0: lambda: sum_out(A), 3: row_out}
            if more:
                pieces[1] = split_x_high
                pieces[2] = lambda: split_x_low(1)
                pieces[8] = lambda: finish_y(1)
                pieces[9] = lambda: split_y_high(2)
                pieces[10] = lambda: (split_y_low(3), nc.vector.sem_clear(s_own))
            return pieces

        def tensor_A(output):
            xs = input_products(B)
            pieces = {2 + k: (lambda: some(xs, 9)) for k in range(4)}
            if output:
                pieces[1] = turn_out
            return pieces

        def vector_A(output):
            if not output:
                return {}

            def keep_y():
                nc.vector.tensor_copy(cols(y_cur[:, :, :, :]), cols(y_new[:, :, :, :])).then_inc(s_own, 1)
                take(nc.vector, s_own, 1)
            return {0: lambda: sum_out(B), 2: keep_y, 3: row_out}

        block = ctx.enter_context(nc.Block())

        @block.sync
        def _(sync):
            sync.dma_start(cond_r[:, :], cond).then_inc(s_cond, 16)
            for n, v in enumerate((ln_g, ln_b, b1)):
                sync.dma_start(vec_r[n * NM:(n + 1) * NM, :], v.rearrange("(m p) -> m p", p=P)).then_inc(s_vec, 16)
            sync.dma_start(w1_f[:, :, :], w1.rearrange("(k p) n -> p k n", p=P)).then_inc(s_w1, 16)
            w2_v = w2.rearrange("(k p) (q n) -> q p k n", p=P, q=4)
            for q in range(4):
                sync.dma_start(w2_f[:, :, q * P * RANK:(q + 1) * P * RANK], w2_v[q]).then_inc(s_w2[q], 16)
            sync.dma_start(base_f[:, :, :], base.rearrange("(k p) n -> p k n", p=P)).then_inc(s_base, 16)
            sync.dma_start(x_in[:, :], x_rows[0:BLOCK]).then_inc(s_xload, 16)
            with sync.Fori(1, NBLOCK) as i:
                sync.wait_ge(s_xfree, i)
                sync.dma_start(x_in[:, :], x_rows[bass.ds(i * BLOCK, BLOCK)]).then_inc(s_xload, 16)

        @block.gpsimd
        def _(pool):
            s_eye = s_ident
            nc.gpsimd.memset(ident[:, :], 0.0).then_inc(s_eye, 1)
            nc.gpsimd.memset(ident16[:, :], 0.0).then_inc(s_eye, 1)
            nc.gpsimd.memset(ones[:, :], 1.0).then_inc(s_ones, 1)
            pool.wait_ge(s_eye, 2)
            for e in (ident, ident16):
                nc.gpsimd.affine_select(out=e[:, :], in_=e[:, :], compare_op=ALU.not_equal, fill=1.0,
                                        base=0, pattern=[[-1, P]], channel_multiplier=1).then_inc(s_eye, 1)
            pool.dma_start(b_row[:, :], b.rearrange("(a n) -> a n", a=1)).then_inc(s_b, 16)
            pool.dma_start(wh_f[:, :, :], wh.rearrange("(k p) n -> p k n", p=P)).then_inc(s_wh, 16)
            pool.dma_start(wx_f[:, :, :], wx.rearrange("(k p) n -> p k n", p=P)).then_inc(s_wx, 16)
            pool.dma_start(b2_c[:, :, :], b2.rearrange("(q p r) -> p q r", q=4, r=RANK)).then_inc(s_b2, 16)
            pool.wait_ge(s_bparts, 1)
            pool.dma_start(b_w[:, :], b_parts[0:1, :, :]).then_inc(s_bw, 16)
            pool.sem_inc(s_ofree, 1)

            def store(q, t0):
                pool.wait_ge(s_orow, q + 1)
                pool.dma_start(out_rows[t0], o_row[:, :]).then_inc(s_store, 16)
                pool.wait_ge(s_store, (q + 1) * 16)
            with pool.Fori(0, NBLOCK - 1) as i:
                for half in range(2):
                    store(i * 2 + half, bass.ds(i * BLOCK + half * HALF, HALF))
                    pool.sem_inc(s_ofree, 1)
            store(2 * NBLOCK - 2, slice(T - BLOCK, T - HALF))
            pool.sem_inc(s_ofree, 1)
            store(2 * NBLOCK - 1, slice(T - HALF, T))

        @block.tensor
        def _(pe):
            pe.wait_ge(s_ident, 4)
            pe.wait_ge(s_cond, 16)
            for k in range(NM):
                nc.tensor.transpose(p_x[:, k * NB:(k + 1) * NB], cond_r[:, k * P:(k + 1) * P], ident[0:NB, 0:NB])
            pe.wait_ge(s_vec, 48)
            nc.tensor.transpose(p_x[:, 64:64 + 3 * NM], vec_r[:, :], ident[0:3 * NM, 0:3 * NM]).then_inc(s_turn0, 1)
            pe.wait_ge(s_norm, 1)
            for k in range(NM):
                last = nc.tensor.transpose(p_y[:, k * NB:(k + 1) * NB], cond_n[:, k * P:(k + 1) * P],
                                           ident[0:NB, 0:NB])
            last.then_inc(s_turn0, 1)
            pe.wait_ge(s_ae, 1)
            pe.wait_ge(s_w1, 16)
            for mo in range(NM):
                for k in range(NM):
                    last = nc.tensor.matmul(p_o[:, mo * NB:(mo + 1) * NB], w1_f[:, k, mo * P:(mo + 1) * P],
                                            ae[:, k, :], start=k == 0, stop=k == NM - 1)
            last.then_inc(s_hmm, 1)
            pe.wait_ge(s_hid, 1)
            for q in range(4):
                pe.wait_ge(s_w2[q], 16)
                for j in range(2):
                    n = 2 * q + j
                    if n >= 4:
                        pe.wait_ge(s_abrow, n - 3)
                    for k in range(NM):
                        last = nc.tensor.matmul(acc[(n // 2) % 2][n % 2][0:NB, :], hid[:, k, :],
                                                w2_f[:, k, n * 512:(n + 1) * 512], start=k == 0, stop=k == NM - 1)
                    last.then_inc(s_abmm, 1)
            for q in range(4):
                pe.wait_ge(s_abrow, 2 * q + 2)
                rows = ab_row[:, q * P * RANK:(q + 1) * P * RANK].rearrange("b (d r) -> b r d", r=RANK)
                for r in range(RANK):
                    c = (q * RANK + r) * NB
                    last = nc.tensor.transpose(p_y[:, 64 + c:64 + c + NB], rows[:, r, :], ident[0:NB, 0:NB])
            last.then_inc(s_abcol, 1)
            pe.wait_ge(s_abst, 1)
            for q in range(4):
                last = nc.tensor.transpose(p_ab[0:NB * 4 * RANK, q * P:(q + 1) * P],
                                           ab_st[:, q].rearrange("p b s r -> p (b s r)"), ident16[:, :])
            last.then_inc(s_abt, 1)
            pe.wait_ge(s_abts, 1)
            for bb in range(NB):
                rows = slice(bb * 4 * RANK, (bb + 1) * 4 * RANK)
                for k in range(NM):
                    last = nc.tensor.matmul(acc[A][bb][:, k * D:(k + 1) * D], ab_t[rows, k, :],
                                            ab_t[rows, 2:4, :].rearrange("p k d -> p (k d)"), start=k == 0, stop=True,
                                            skip_group_check=True)
                last.then_inc(s_lmm, 1)
            turn_x()
            take(pe, s_xsplit, 1)
            pe.wait_ge(s_layer, 2)
            some(layer_products(), 100).then_inc(s_ymm, 1)
            take(pe, s_ysplit, 1)
            pe.wait_ge(s_split, 2)
            pe.wait_ge(s_bw, 16)
            pe.wait_ge(s_ones, 1)
            some(input_products(A), 100)
            tensor_half(A, tensor_A(False))
            with pe.Fori(0, NBLOCK - 1) as i:
                tensor_half(B, tensor_B(True))
                tensor_half(A, tensor_A(True))
            tensor_half(B, tensor_B(False))
            turn_out()

        @block.scalar
        def _(act):
            act.wait_ge(s_var, 1)
            nc.scalar.activation(rstd[:, 1:2], veps[:, :], ACT.Sqrt).then_inc(s_sqrt, 1)
            act.wait_ge(s_wh, 16)
            nc.scalar.activation(wh_s[:, 0].rearrange("p k n -> p (k n)"), wh_f[:, :, :].rearrange("p k n -> p (k n)"),
                                 ACT.Copy, scale=SCALE).then_inc(s_hi, 1)
            act.wait_ge(s_wx, 16)
            nc.scalar.activation(wx_s[:, 0].rearrange("p k n -> p (k n)"), wx_f[:, :, :].rearrange("p k n -> p (k n)"),
                                 ACT.Copy, scale=SCALE).then_inc(s_hi, 1)
            act.wait_ge(s_hmm, 1)
            act.wait_ge(s_vecc, 1)
            for m in range(NM):
                last = nc.scalar.activation(hid[:, m, :], p_o[:, m * NB:(m + 1) * NB], ACT.Gelu,
                                            bias=vec_c[:, 2, m:m + 1])
            last.then_inc(s_hid, 1)
            for n in range(8):
                act.wait_ge(s_abmm, n + 1)
                nc.scalar.copy(ab_row[:, n * 512:(n + 1) * 512], acc[(n // 2) % 2][n % 2][0:NB, :]).then_inc(s_abrow, 1)
            for bb in range(NB):
                act.wait_ge(s_lay, bb + 1)
                nc.scalar.copy(lay_s[:, 0, bb].rearrange("p k n -> p (k n)"),
                               lay_f[:, bb].rearrange("p k n -> p (k n)")).then_inc(s_layhi, 1)
            act.wait_ge(s_condc, 1)
            give_h(0, cond_c[:, :], ACT.Copy, 1.0)
            scalar_half(A)
            with act.Fori(0, NBLOCK - 1) as i:
                scalar_half(B)
                scalar_half(A)
            scalar_half(B, final=True)

        @block.vector
        def _(dve):
            count = [0]

            def linked(ins):
                count[0] += 1
                ins.then_inc(s_link, 1)
                dve.wait_ge(s_link, count[0])

            dve.wait_ge(s_cond, 16)
            linked(nc.vector.bn_stats(stats[:, :], cond_r[:, :]))
            linked(nc.vector.bn_aggr(mv[:, :], stats[:, :]))
            linked(nc.vector.tensor_scalar(veps[:, :], mv[:, 1:2], LN_EPS, None, ALU.add))
            dve.sem_inc(s_var, 1)
            dve.wait_ge(s_sqrt, 1)
            linked(nc.vector.reciprocal(rstd[:, 0:1], rstd[:, 1:2]))
            linked(nc.vector.tensor_scalar(rstd[:, 1:2], rstd[:, 0:1], rstd[:, 0:1], veps[:, 0:1], ALU.mult, ALU.mult))
            linked(nc.vector.tensor_scalar(rstd[:, 1:2], rstd[:, 1:2], -0.5, 1.5, ALU.mult, ALU.add))
            linked(nc.vector.tensor_mul(rstd[:, 0:1], rstd[:, 0:1], rstd[:, 1:2]))
            nc.vector.tensor_scalar(cond_n[:, :], cond_r[:, :], mv[:, 0:1], rstd[:, 0:1],
                                    ALU.subtract, ALU.mult).then_inc(s_norm, 1)
            dve.wait_ge(s_turn0, 1)
            nc.vector.tensor_copy(cond_c[:, :], p_x[:, 0:COLS]).then_inc(s_condc, 1)
            nc.vector.tensor_copy(vec_c[:, :, :].rearrange("p v m -> p (v m)"),
                                  p_x[:, 64:64 + 3 * NM]).then_inc(s_vecc, 1)
            dve.wait_ge(s_vecc, 1)
            dve.wait_ge(s_turn0, 2)
            for k in range(NM):
                last = nc.vector.tensor_scalar(ae[:, k, :], p_y[:, k * NB:(k + 1) * NB], vec_c[:, 0, k:k + 1],
                                               vec_c[:, 1, k:k + 1], ALU.mult, ALU.add)
            last.then_inc(s_ae, 1)
            for n, (src, dst, s) in enumerate(((wh_f, wh_s, s_wh), (wx_f, wx_s, s_wx))):
                dve.wait_ge(s, 16)
                dve.wait_ge(s_hi, n + 1)
                nc.vector.scalar_tensor_tensor(
                    dst[:, 1].rearrange("p k n -> p (k n)"), src[:, :, :].rearrange("p k n -> p (k n)"), SCALE,
                    dst[:, 0].rearrange("p k n -> p (k n)"), ALU.mult, ALU.subtract).then_inc(s_split, 1)
            dve.wait_ge(s_b, 16)
            linked(nc.vector.tensor_scalar(b_row[:, :], b_row[:, :], SCALE, None, ALU.mult))
            linked(nc.vector.tensor_copy(b_parts[:, 0, :], b_row[:, :]))
            linked(nc.vector.tensor_sub(b_rest[:, :], b_row[:, :], b_parts[:, 0, :]))
            linked(nc.vector.tensor_copy(b_parts[:, 1, :], b_rest[:, :]))
            nc.vector.tensor_sub(b_parts[:, 2, :], b_rest[:, :], b_parts[:, 1, :]).then_inc(s_bparts, 1)
            dve.wait_ge(s_b2, 16)
            dve.wait_ge(s_abcol, 1)
            pab = p_y[:, 64:64 + 4 * RANK * NB].rearrange("p (q r b) -> p b (q r)", r=RANK, b=NB)
            abf = ab_f[:, :, :, :].rearrange("p q b r -> p b q r")
            for bb in range(NB):
                last = nc.vector.tensor_add(abf[:, bb], pab[:, bb].rearrange("p (q r) -> p q r", r=RANK), b2_c[:, :, :])
            linked(last)
            HI = {0: (0, 1), 1: (0, 2)}
            LO = {0: (2, 3), 1: (1, 3)}
            for ab in range(2):
                q = slice(2 * ab, 2 * ab + 2)
                for part in HI[ab]:
                    for bb in range(NB):
                        last = nc.vector.tensor_copy(ab_st[:, q, bb, part, :], ab_f[:, q, bb, :])
            linked(last)
            for ab in range(2):
                q = slice(2 * ab, 2 * ab + 2)
                for part in LO[ab]:
                    for bb in range(NB):
                        last = nc.vector.tensor_sub(ab_st[:, q, bb, part, :], ab_f[:, q, bb, :], ab_st[:, q, bb, 0, :])
            last.then_inc(s_abst, 1)
            dve.wait_ge(s_abt, 1)
            nc.vector.tensor_copy(ab_t[:, :, :].rearrange("p q d -> p (q d)"),
                                  p_ab[0:NB * 4 * RANK, :]).then_inc(s_abts, 1)
            dve.wait_ge(s_base, 16)
            for bb in range(NB):
                dve.wait_ge(s_lmm, bb + 1)
                nc.vector.tensor_add(lay_f[:, bb].rearrange("p k n -> p (k n)"),
                                     base_f[:, :, :].rearrange("p k n -> p (k n)"), acc[A][bb][:, :]).then_inc(s_lay, 1)
            for bb in range(NB):
                dve.wait_ge(s_layhi, bb + 1)
                nc.vector.tensor_sub(lay_s[:, 1, bb].rearrange("p k n -> p (k n)"),
                                     lay_f[:, bb].rearrange("p k n -> p (k n)"),
                                     lay_s[:, 0, bb].rearrange("p k n -> p (k n)")).then_inc(s_layer, 1)
            split_x_high()
            split_x_low(1)
            finish_y(1)
            split_y_high(2)
            split_y_low(3)
            linked(nc.vector.tensor_copy(cols(y_cur[:, :, :, :]), cols(y_new[:, :, :, :])))
            dve.sem_clear(s_own)
            vector_half(A, vector_A(False))
            with dve.Fori(0, NBLOCK - 1) as i:
                vector_half(B, vector_B(True))
                vector_half(A, vector_A(True))
            vector_half(B, vector_B(False))
            dve.wait_ge(s_hf[A], 1)
            sum_out(B)
            row_out()


def kernel(x, cond_1024, L0_cond_base_layer, L0_cond_w1, L0_cond_b1, L0_cond_w2, L0_cond_b2, L0_cond_ln_g,
           L0_cond_ln_b, L1_cond_Wx, L1_cond_Wh, L1_cond_b):
    import concourse.bacc as bacc
    from concourse.bass_utils import run_bass_kernel_spmd

    ins = dict(x=x, cond=cond_1024, base=L0_cond_base_layer, w1=L0_cond_w1, b1=L0_cond_b1, w2=L0_cond_w2,
               b2=L0_cond_b2, ln_g=L0_cond_ln_g, ln_b=L0_cond_ln_b, wx=L1_cond_Wx, wh=L1_cond_Wh, b=L1_cond_b)
    nc = bacc.Bacc("TRN2", target_bir_lowering=False, num_devices=1)
    arrays, args = {}, {}
    for name, a in ins.items():
        a = np.ascontiguousarray(a)
        arrays[f"{name}_dram"] = a
        args[name] = nc.dram_tensor(f"{name}_dram", a.shape, mybir.dt.from_np(a.dtype), kind="ExternalInput").ap()
    args["out"] = nc.dram_tensor("out_dram", (NB, T, D), F32, kind="ExternalOutput").ap()
    cond_recurrence(nc, **args)
    r = run_bass_kernel_spmd(nc, [arrays], core_ids=[0])
    return r.results[0]["out_dram"]
```

```python
from contextlib import ExitStack

import numpy as np
import concourse.bass as bass
from concourse import mybir

F32, F16 = mybir.dt.float32, mybir.dt.float16
ACT, ALU = mybir.ActivationFunctionType, mybir.AluOpType

P = 128
NB = 2
T = 1024
D = 256
NM = D // P
RANK = 8
COLS = NM * NB
BLOCK = 32
HALF = BLOCK // 2
NBLOCK = T // BLOCK
PAIRS = HALF // 2
SCALE = 256.0
LN_EPS = 1e-5
A, B = 0, 1


def cond_recurrence(nc, x, cond, base, w1, b1, w2, b2, ln_g, ln_b, wx, wh, b, out):
    ctx = ExitStack()
    with ctx:
        def sb(name, shape, dt=F32):
            return ctx.enter_context(nc.sbuf_tensor(name, shape, dt))

        def pb(name, shape, dt=F32):
            return ctx.enter_context(nc.psum_tensor(name, shape, dt))

        def sem(name):
            return ctx.enter_context(nc.semaphore(name))

        ident = sb("ident", [P, P])
        ident16 = sb("ident16", [P, P], F16)
        wh_f = sb("wh_f", [P, NM, D])
        wx_f = sb("wx_f", [P, NM, D])
        base_f = sb("base_f", [P, NM, D])
        w1_f = sb("w1_f", [P, NM, D])
        w2_f = sb("w2_f", [P, NM, 2 * D * RANK])
        wh_s = sb("wh_s", [P, 2, NM, D], F16)
        wx_s = sb("wx_s", [P, 2, NM, D], F16)
        lay_f = sb("lay_f", [P, NB, NM, D])
        lay_s = sb("lay_s", [P, 2, NB, NM, D], F16)
        b_row = sb("b_row", [1, D])
        b_rest = sb("b_rest", [1, D])
        b_parts = sb("b_parts", [1, 3, D], F16)
        b_w = sb("b_w", [3, D], F16)
        ones = sb("ones", [3, PAIRS * NB], F16)
        cond_r = sb("cond_r", [NB, D])
        cond_n = sb("cond_n", [NB, D])
        cond_c = sb("cond_c", [P, COLS])
        stats = sb("stats", [NB, 6])
        mv = sb("mv", [NB, 2])
        veps = sb("veps", [NB, 1])
        rstd = sb("rstd", [NB, 2])
        warm = sb("warm", [NB, 1])
        vec_r = sb("vec_r", [3 * NM, P])
        vec_c = sb("vec_c", [P, 3, NM])
        ae = sb("ae", [P, NM, NB])
        hid = sb("hid", [P, NM, NB])
        hid_s = sb("hid_s", [P, NM, 2, NB], F16)
        w2_s = sb("w2_s", [P, 2, NM, 2 * D * RANK], F16)
        ab_sum = sb("ab_sum", [P, 4, RANK, NB])
        b2_c = sb("b2_c", [P, 4, RANK])
        ab_f = sb("ab_f", [P, 4, NB, RANK])
        ab_st = sb("ab_st", [P, 4, NB, 4, RANK], F16)
        ab_t = sb("ab_t", [NB * 4 * RANK, 4, P], F16)
        x_in = sb("x_in", [P, P])
        x_f = sb("x_f", [P, BLOCK, NM, NB])
        x_s = sb("x_s", [P, 2, BLOCK, NM, NB], F16)
        y_new = sb("y_new", [P, BLOCK, NM, NB])
        y_cur = sb("y_cur", [P, BLOCK, NM, NB])
        y_s = sb("y_s", [P, 2, BLOCK, NM, NB], F16)
        h_f = sb("h_f", [P, BLOCK, COLS])
        h_hi = sb("h_hi", [P, 2, NM, NB], F16)
        h_lo = sb("h_lo", [P, 2, NM, NB], F16)
        o_sum = sb("o_sum", [P, HALF * COLS])
        o_row = sb("o_row", [HALF * COLS, P])

        acc = [[pb(f"acc{half}{par}", [P, 512]) for par in range(2)] for half in range(2)]
        p_x = pb("p_x", [P, 512])
        p_y = pb("p_y", [P, 512])
        p_o = pb("p_o", [P, 512])
        p_ab = pb("p_ab", [P, 4 * P], F16)

        s_cond, s_vec, s_w1, s_b2, s_base = sem("s_cond"), sem("s_vec"), sem("s_w1"), sem("s_b2"), sem("s_base")
        s_w2 = [sem(f"s_w2_{n}") for n in range(4 * NM)]
        s_wh, s_wx, s_b, s_bw = sem("s_wh"), sem("s_wx"), sem("s_b"), sem("s_bw")
        s_ident = sem("s_ident")
        s_ones = sem("s_ones")
        s_hi = sem("s_hi")
        s_split = sem("s_split")
        s_bparts = sem("s_bparts")
        s_var = sem("s_var")
        s_sqrt = sem("s_sqrt")
        s_norm = sem("s_norm")
        s_turn0 = sem("s_turn0")
        s_condc = sem("s_condc")
        s_vecc = sem("s_vecc")
        s_ae = sem("s_ae")
        s_hmm = sem("s_hmm")
        s_hid = sem("s_hid")
        s_hidhi = sem("s_hidhi")
        s_w2hi = sem("s_w2hi")
        s_w2lo = sem("s_w2lo")
        s_abcol = sem("s_abcol")
        s_abst = sem("s_abst")
        s_abt = sem("s_abt")
        s_abts = sem("s_abts")
        s_lmm = sem("s_lmm")
        s_lay = sem("s_lay")
        s_layhi = sem("s_layhi")
        s_layer = sem("s_layer")
        s_link = sem("s_link")
        s_sum = [sem("s_sumA"), sem("s_sumB")]
        s_hhi = [sem("s_hhiA"), sem("s_hhiB")]
        s_hf = [sem("s_hfA"), sem("s_hfB")]
        s_hlo = [sem("s_hloA"), sem("s_hloB")]
        s_xload = sem("s_xload")
        s_xfree = sem("s_xfree")
        s_xturn = sem("s_xturn")
        s_xsplit = sem("s_xsplit")
        s_ymm = sem("s_ymm")
        s_ysplit = sem("s_ysplit")
        s_osum = sem("s_osum")
        s_oturn = sem("s_oturn")
        s_orow = sem("s_orow")
        s_store = sem("s_store")
        s_ofree = sem("s_ofree")
        s_own = sem("s_own")

        W2_PIECES = [(q, k) for q in range(4) for k in range(NM)]

        def tile_of_ab(q):
            return slice(q * P * RANK, (q + 1) * P * RANK)

        x_rows = x.rearrange("b t (m p) -> t m b p", p=P)
        out_rows = out.rearrange("b t (m p) -> t m b p", p=P)
        cols = lambda ap: ap.rearrange("p t m b -> p (t m b)")

        def take(eng, s, n):
            eng.wait_ge(s, n)
            eng.sem_clear(s)

        def turn_x():
            take(nc.tensor, s_xload, 16)
            nc.tensor.transpose(p_x[:, 0:P], x_in[:, :], ident[:, :]).then_inc(s_xturn, 1)

        PARTS = [(0, 0), (1, 0), (0, 1), (1, 1)]

        def layer_products():
            first = True
            todo = [(bb, mo, ki, pw, px) for bb in range(NB) for mo in range(NM)
                    for ki in range(NM) for pw, px in PARTS]
            py = p_y[:, 0:P].rearrange("p (t m b) -> p t m b", m=NM, b=NB)
            for bb, mo, ki, pw, px in todo:
                yield nc.tensor.matmul(py[:, :, mo, bb], lay_s[:, pw, bb, ki, mo * P:(mo + 1) * P],
                                       x_s[:, px, :, ki, bb], start=first, stop=True, skip_group_check=True)
                first = False

        def input_products(half):
            for par in range(2):
                av = acc[half][par][:, 0:PAIRS * COLS].rearrange("p (t m b) -> p t m b", m=NM, b=NB)
                for mo in range(NM):
                    yield nc.tensor.matmul(av[:, :, mo, :], b_w[:, mo * P:(mo + 1) * P], ones[:, :],
                                           start=mo == 0, stop=True, skip_group_check=True)
                for mo in range(NM):
                    for ki in range(NM):
                        for pw, py in PARTS:
                            t0 = half * HALF + par
                            yield nc.tensor.matmul(
                                av[:, :, mo, :], wx_s[:, pw, ki, mo * P:(mo + 1) * P],
                                y_s[:, py, t0:t0 + HALF - 1:2, ki, :],
                                start=False, stop=True, skip_group_check=True)

        def some(products, n):
            last = None
            for _ in range(n):
                nxt = next(products, None)
                last = nxt if nxt is not None else last
            return last

        def turn_out():
            take(nc.tensor, s_osum, 1)
            nc.tensor.transpose(p_o[0:HALF * COLS, 0:P], o_sum[:, :], ident[:, :]).then_inc(s_oturn, 1)

        def split_x_high():
            take(nc.vector, s_xturn, 1)
            nc.vector.tensor_copy(cols(x_f[:, :, :, :]), p_x[:, 0:P]).then_inc(s_xfree, 1)
            nc.vector.tensor_copy(cols(x_s[:, 0]), p_x[:, 0:P]).then_inc(s_own, 1)

        def split_x_low(own):
            nc.vector.wait_ge(s_own, own)
            nc.vector.tensor_sub(cols(x_s[:, 1]), p_x[:, 0:P], cols(x_s[:, 0])).then_inc(s_xsplit, 1)

        def finish_y(own):
            take(nc.vector, s_ymm, 1)
            nc.vector.scalar_tensor_tensor(cols(y_new[:, :, :, :]), cols(x_f[:, :, :, :]), 2.0, p_y[:, 0:P],
                                           ALU.mult, ALU.add).then_inc(s_own, 1)

        def split_y_high(own):
            nc.vector.wait_ge(s_own, own)
            nc.vector.tensor_copy(cols(y_s[:, 0]), cols(y_new[:, :, :, :])).then_inc(s_own, 1)

        def split_y_low(own):
            nc.vector.wait_ge(s_own, own)
            nc.vector.tensor_sub(cols(y_s[:, 1]), cols(y_new[:, :, :, :]), cols(y_s[:, 0])).then_inc(s_ysplit, 1)

        def sum_out(half):
            sl = slice(half * HALF, (half + 1) * HALF)
            nc.vector.tensor_add(o_sum[:, :], cols(y_cur[:, sl]),
                                 h_f[:, sl, :].rearrange("p t c -> p (t c)")).then_inc(s_osum, 1)

        def row_out():
            take(nc.vector, s_oturn, 1)
            take(nc.vector, s_ofree, 1)
            nc.vector.tensor_copy(o_row[:, :], p_o[0:HALF * COLS, 0:P]).then_inc(s_orow, 1)

        def tensor_half(half, pieces):
            for u in range(HALF):
                par = u % 2
                dst = acc[half][par][:, (u // 2) * COLS:(u // 2 + 1) * COLS]
                nc.tensor.wait_ge(s_hhi[half], u + 1)
                for pw in range(2):
                    for mo in range(NM):
                        for ki in range(NM):
                            nc.tensor.matmul(dst[:, mo * NB:(mo + 1) * NB], wh_s[:, pw, ki, mo * P:(mo + 1) * P],
                                             h_hi[:, par, ki, :], start=False, stop=True, skip_group_check=True)
                nc.tensor.wait_ge(s_hlo[half], u + 1)
                for mo in range(NM):
                    for ki in range(NM):
                        last = nc.tensor.matmul(dst[:, mo * NB:(mo + 1) * NB], wh_s[:, 0, ki, mo * P:(mo + 1) * P],
                                                h_lo[:, par, ki, :], start=False, stop=True, skip_group_check=True)
                last.then_inc(s_sum[half], 1)
                if u in pieces:
                    pieces[u]()
            nc.tensor.sem_clear(s_hhi[half])
            nc.tensor.sem_clear(s_hlo[half])

        def give_h(n, src, func, scale, final=False):
            half, par, slot = (n // HALF) % 2, n % 2, (n - 1) % BLOCK
            if not final:
                nc.scalar.activation(h_hi[:, par].rearrange("p m b -> p (m b)"), src, func,
                                     scale=scale).then_inc(s_hhi[half], 1)
            nc.scalar.activation(h_f[:, slot, :], src, func, scale=scale).then_inc(s_hf[half], 1)

        def scalar_half(half, final=False):
            for u in range(HALF):
                nc.scalar.wait_ge(s_sum[half], u + 1)
                give_h(half * HALF + u + 1, acc[half][u % 2][:, (u // 2) * COLS:(u // 2 + 1) * COLS],
                       ACT.Tanh, 1.0 / SCALE, final=final and u == HALF - 1)
            nc.scalar.sem_clear(s_sum[half])

        def vector_half(half, pieces):
            for u in range(HALF):
                par, slot = u % 2, (half * HALF + u - 1) % BLOCK
                nc.vector.wait_ge(s_hf[half], u + 1)
                nc.vector.tensor_sub(h_lo[:, par].rearrange("p m b -> p (m b)"), h_f[:, slot, :],
                                     h_hi[:, par].rearrange("p m b -> p (m b)")).then_inc(s_hlo[half], 1)
                if u in pieces:
                    pieces[u]()
            nc.vector.sem_clear(s_hf[half])

        def tensor_B(more):
            ps, xs = layer_products(), input_products(A)
            pieces = {1: turn_out}
            if more:
                def turn():
                    turn_x()
                def y_part(n, wait, end):
                    def piece():
                        if wait:
                            take(nc.tensor, s_xsplit, 1)
                        last = some(ps, n)
                        if end:
                            last.then_inc(s_ymm, 1)
                    return piece
                def acc_part(n, wait):
                    def piece():
                        if wait:
                            take(nc.tensor, s_ysplit, 1)
                        some(xs, n)
                    return piece
                pieces[0] = turn
                for k in range(4):
                    pieces[4 + k] = y_part(8, k == 0, k == 3)
                for k in range(4):
                    pieces[12 + k] = acc_part(9, k == 0)
            return pieces

        def vector_B(more):
            pieces = {0: lambda: sum_out(A), 3: row_out}
            if more:
                pieces[1] = split_x_high
                pieces[2] = lambda: split_x_low(1)
                pieces[8] = lambda: finish_y(1)
                pieces[9] = lambda: split_y_high(2)
                pieces[10] = lambda: (split_y_low(3), nc.vector.sem_clear(s_own))
            return pieces

        def tensor_A(output):
            xs = input_products(B)
            pieces = {2 + k: (lambda: some(xs, 9)) for k in range(4)}
            if output:
                pieces[1] = turn_out
            return pieces

        def vector_A(output):
            if not output:
                return {}

            def keep_y():
                nc.vector.tensor_copy(cols(y_cur[:, :, :, :]), cols(y_new[:, :, :, :])).then_inc(s_own, 1)
                take(nc.vector, s_own, 1)
            return {0: lambda: sum_out(B), 2: keep_y, 3: row_out}

        block = ctx.enter_context(nc.Block())

        @block.sync
        def _(sync):
            sync.dma_start(cond_r[:, :], cond).then_inc(s_cond, 16)
            for n, v in enumerate((ln_g, ln_b, b1)):
                sync.dma_start(vec_r[n * NM:(n + 1) * NM, :], v.rearrange("(m p) -> m p", p=P)).then_inc(s_vec, 16)
            sync.dma_start(w1_f[:, :, :], w1.rearrange("(k p) n -> p k n", p=P)).then_inc(s_w1, 16)
            for n, (q, k) in enumerate(W2_PIECES):
                sync.dma_start(w2_f[:, k, tile_of_ab(q)], w2[k * P:(k + 1) * P, tile_of_ab(q)]).then_inc(s_w2[n], 16)
            sync.dma_start(base_f[:, :, :], base.rearrange("(k p) n -> p k n", p=P)).then_inc(s_base, 16)
            sync.dma_start(x_in[:, :], x_rows[0:BLOCK]).then_inc(s_xload, 16)
            sync.wait_ge(s_xfree, 1)
            sync.dma_start(x_in[:, :], x_rows[BLOCK:2 * BLOCK]).then_inc(s_xload, 16)
            sync.sem_inc(s_ofree, 1)

            def store(q, t0, more=True):
                sync.wait_ge(s_orow, q + 1)
                sync.dma_start(out_rows[t0], o_row[:, :]).then_inc(s_store, 16)
                sync.wait_ge(s_store, (q + 1) * 16)
                if more:
                    sync.sem_inc(s_ofree, 1)

            with sync.Fori(0, NBLOCK - 2) as i:
                sync.wait_ge(s_xfree, i + 2)
                sync.dma_start(x_in[:, :], x_rows[bass.ds((i + 2) * BLOCK, BLOCK)]).then_inc(s_xload, 16)
                for half in range(2):
                    store(i * 2 + half, bass.ds(i * BLOCK + half * HALF, HALF))
            for q in range(2 * (NBLOCK - 2), 2 * NBLOCK):
                store(q, slice(q * HALF, (q + 1) * HALF), more=q < 2 * NBLOCK - 1)

        @block.gpsimd
        def _(pool):
            s_eye = s_ident
            nc.gpsimd.memset(ident[:, :], 0.0).then_inc(s_eye, 1)
            nc.gpsimd.memset(ident16[:, :], 0.0).then_inc(s_eye, 1)
            nc.gpsimd.memset(ones[:, :], 1.0).then_inc(s_ones, 1)
            pool.wait_ge(s_eye, 2)
            for e in (ident, ident16):
                nc.gpsimd.affine_select(out=e[:, :], in_=e[:, :], compare_op=ALU.not_equal, fill=1.0,
                                        base=0, pattern=[[-1, P]], channel_multiplier=1).then_inc(s_eye, 1)
            pool.dma_start(b_row[:, :], b.rearrange("(a n) -> a n", a=1)).then_inc(s_b, 16)
            pool.dma_start(wh_f[:, :, :], wh.rearrange("(k p) n -> p k n", p=P)).then_inc(s_wh, 16)
            pool.dma_start(wx_f[:, :, :], wx.rearrange("(k p) n -> p k n", p=P)).then_inc(s_wx, 16)
            pool.dma_start(b2_c[:, :, :], b2.rearrange("(q p r) -> p q r", q=4, r=RANK)).then_inc(s_b2, 16)
            def step(n, ins):
                ins.then_inc(s_bparts, 1)
                pool.wait_ge(s_bparts, n)
            pool.wait_ge(s_b, 16)
            step(1, nc.gpsimd.tensor_scalar(b_row[:, :], b_row[:, :], SCALE, None, ALU.mult))
            step(2, nc.gpsimd.tensor_copy(b_parts[:, 0, :], b_row[:, :]))
            step(3, nc.gpsimd.tensor_sub(b_rest[:, :], b_row[:, :], b_parts[:, 0, :]))
            step(4, nc.gpsimd.tensor_copy(b_parts[:, 1, :], b_rest[:, :]))
            step(5, nc.gpsimd.tensor_sub(b_parts[:, 2, :], b_rest[:, :], b_parts[:, 1, :]))
            pool.dma_start(b_w[:, :], b_parts[0:1, :, :]).then_inc(s_bw, 16)

        @block.tensor
        def _(pe):
            pe.wait_ge(s_ident, 4)
            pe.wait_ge(s_cond, 16)
            for k in range(NM):
                nc.tensor.transpose(p_x[:, k * NB:(k + 1) * NB], cond_r[:, k * P:(k + 1) * P], ident[0:NB, 0:NB])
            pe.wait_ge(s_vec, 48)
            nc.tensor.transpose(p_x[:, 64:64 + 3 * NM], vec_r[:, :], ident[0:3 * NM, 0:3 * NM]).then_inc(s_turn0, 1)
            pe.wait_ge(s_norm, 1)
            for k in range(NM):
                last = nc.tensor.transpose(p_y[:, k * NB:(k + 1) * NB], cond_n[:, k * P:(k + 1) * P],
                                           ident[0:NB, 0:NB])
            last.then_inc(s_turn0, 1)
            pe.wait_ge(s_ae, 1)
            pe.wait_ge(s_w1, 16)
            for mo in range(NM):
                for k in range(NM):
                    last = nc.tensor.matmul(p_o[:, mo * NB:(mo + 1) * NB], w1_f[:, k, mo * P:(mo + 1) * P],
                                            ae[:, k, :], start=k == 0, stop=k == NM - 1)
            last.then_inc(s_hmm, 1)
            pe.wait_ge(s_hid, 1)
            for n, (q, k) in enumerate(W2_PIECES):
                if n == 6:
                    turn_x()
                for pw, ready in ((0, s_w2hi), (1, s_w2lo)):
                    pe.wait_ge(ready, n + 1)
                    for r in range(RANK):
                        c = 64 + (q * RANK + r) * 2 * NB
                        w = w2_s[:, pw, k, tile_of_ab(q)].rearrange("p (d r) -> p r d", r=RANK)
                        last = nc.tensor.matmul(p_y[:, c:c + 2 * NB], w[:, r, :],
                                                hid_s[:, k].rearrange("p s b -> p (s b)"),
                                                start=n == 0 and pw == 0 and r == 0, stop=True, skip_group_check=True)
            last.then_inc(s_abcol, 1)
            pe.wait_ge(s_abst, 1)
            for q in range(4):
                last = nc.tensor.transpose(p_ab[0:NB * 4 * RANK, q * P:(q + 1) * P],
                                           ab_st[:, q].rearrange("p b s r -> p (b s r)"), ident16[:, :])
            last.then_inc(s_abt, 1)
            pe.wait_ge(s_abts, 1)
            for bb in range(NB):
                rows = slice(bb * 4 * RANK, (bb + 1) * 4 * RANK)
                for k in range(NM):
                    last = nc.tensor.matmul(acc[A][bb][:, k * D:(k + 1) * D], ab_t[rows, k, :],
                                            ab_t[rows, 2:4, :].rearrange("p k d -> p (k d)"), start=k == 0, stop=True,
                                            skip_group_check=True)
                last.then_inc(s_lmm, 1)
            take(pe, s_xsplit, 1)
            pe.wait_ge(s_layer, 2)
            some(layer_products(), 100).then_inc(s_ymm, 1)
            take(pe, s_ysplit, 1)
            pe.wait_ge(s_split, 2)
            pe.wait_ge(s_bw, 16)
            pe.wait_ge(s_ones, 1)
            some(input_products(A), 100)
            tensor_half(A, tensor_A(False))
            with pe.Fori(0, NBLOCK - 1) as i:
                tensor_half(B, tensor_B(True))
                tensor_half(A, tensor_A(True))
            tensor_half(B, tensor_B(False))
            turn_out()

        @block.scalar
        def _(act):
            act.wait_ge(s_var, 1)
            nc.scalar.activation(rstd[:, 1:2], veps[:, :], ACT.Sqrt).then_inc(s_sqrt, 1)
            nc.scalar.activation(warm[:, :], veps[:, :], ACT.Gelu)
            act.wait_ge(s_hmm, 1)
            act.wait_ge(s_vecc, 1)
            for m in range(NM):
                for dst in (hid_s[:, m, 0, :], hid[:, m, :]):
                    last = nc.scalar.activation(dst, p_o[:, m * NB:(m + 1) * NB], ACT.Gelu, bias=vec_c[:, 2, m:m + 1])
            last.then_inc(s_hidhi, 1)

            def high(dst, src, s):
                act.wait_ge(s, 16)
                nc.scalar.activation(dst[:, 0].rearrange("p k n -> p (k n)"),
                                     src[:, :, :].rearrange("p k n -> p (k n)"), ACT.Copy,
                                     scale=SCALE).then_inc(s_hi, 1)

            for n, (q, k) in enumerate(W2_PIECES):
                act.wait_ge(s_w2[n], 16)
                nc.scalar.copy(w2_s[:, 0, k, tile_of_ab(q)], w2_f[:, k, tile_of_ab(q)]).then_inc(s_w2hi, 1)
                if n == 1:
                    high(wh_s, wh_f, s_wh)
                if n == 5:
                    high(wx_s, wx_f, s_wx)
            for bb in range(NB):
                act.wait_ge(s_lay, bb + 1)
                nc.scalar.copy(lay_s[:, 0, bb].rearrange("p k n -> p (k n)"),
                               lay_f[:, bb].rearrange("p k n -> p (k n)")).then_inc(s_layhi, 1)
            act.wait_ge(s_condc, 1)
            give_h(0, cond_c[:, :], ACT.Copy, 1.0)
            scalar_half(A)
            with act.Fori(0, NBLOCK - 1) as i:
                scalar_half(B)
                scalar_half(A)
            scalar_half(B, final=True)

        @block.vector
        def _(dve):
            count = [0]

            def linked(ins):
                count[0] += 1
                ins.then_inc(s_link, 1)
                dve.wait_ge(s_link, count[0])

            dve.wait_ge(s_cond, 16)
            linked(nc.vector.bn_stats(stats[:, :], cond_r[:, :]))
            linked(nc.vector.bn_aggr(mv[:, :], stats[:, :]))
            linked(nc.vector.tensor_scalar(veps[:, :], mv[:, 1:2], LN_EPS, None, ALU.add))
            dve.sem_inc(s_var, 1)
            dve.wait_ge(s_sqrt, 1)
            linked(nc.vector.reciprocal(rstd[:, 0:1], rstd[:, 1:2]))
            linked(nc.vector.tensor_scalar(rstd[:, 1:2], rstd[:, 0:1], rstd[:, 0:1], veps[:, 0:1], ALU.mult, ALU.mult))
            linked(nc.vector.tensor_scalar(rstd[:, 1:2], rstd[:, 1:2], -0.5, 1.5, ALU.mult, ALU.add))
            linked(nc.vector.tensor_mul(rstd[:, 0:1], rstd[:, 0:1], rstd[:, 1:2]))
            nc.vector.tensor_scalar(cond_n[:, :], cond_r[:, :], mv[:, 0:1], rstd[:, 0:1],
                                    ALU.subtract, ALU.mult).then_inc(s_norm, 1)
            dve.wait_ge(s_turn0, 1)
            nc.vector.tensor_copy(cond_c[:, :], p_x[:, 0:COLS]).then_inc(s_condc, 1)
            nc.vector.tensor_copy(vec_c[:, :, :].rearrange("p v m -> p (v m)"),
                                  p_x[:, 64:64 + 3 * NM]).then_inc(s_vecc, 1)
            dve.wait_ge(s_vecc, 1)
            dve.wait_ge(s_turn0, 2)
            for k in range(NM):
                last = nc.vector.tensor_scalar(ae[:, k, :], p_y[:, k * NB:(k + 1) * NB], vec_c[:, 0, k:k + 1],
                                               vec_c[:, 1, k:k + 1], ALU.mult, ALU.add)
            last.then_inc(s_ae, 1)
            dve.wait_ge(s_hidhi, 1)
            nc.vector.tensor_sub(hid_s[:, :, 1, :], hid[:, :, :], hid_s[:, :, 0, :]).then_inc(s_hid, 1)

            def low(dst, src, n):
                dve.wait_ge(s_hi, n + 1)
                nc.vector.scalar_tensor_tensor(
                    dst[:, 1].rearrange("p k n -> p (k n)"), src[:, :, :].rearrange("p k n -> p (k n)"), SCALE,
                    dst[:, 0].rearrange("p k n -> p (k n)"), ALU.mult, ALU.subtract).then_inc(s_split, 1)

            for n, (q, k) in enumerate(W2_PIECES):
                dve.wait_ge(s_w2hi, n + 1)
                nc.vector.tensor_sub(w2_s[:, 1, k, tile_of_ab(q)], w2_f[:, k, tile_of_ab(q)],
                                     w2_s[:, 0, k, tile_of_ab(q)]).then_inc(s_w2lo, 1)
                if n == 2:
                    low(wh_s, wh_f, 0)
                if n == 6:
                    low(wx_s, wx_f, 1)
            split_x_high()
            split_x_low(1)
            dve.wait_ge(s_b2, 16)
            dve.wait_ge(s_abcol, 1)
            pab = p_y[:, 64:64 + 4 * RANK * 2 * NB].rearrange("p (c s b) -> p s c b", s=2, b=NB)
            linked(nc.vector.tensor_add(ab_sum[:, :, :, :].rearrange("p q r b -> p (q r) b"), pab[:, 1],
                                        b2_c[:, :, :].rearrange("p q r -> p (q r)").unsqueeze(2)
                                        .broadcast_to([P, 4 * RANK, NB])))
            for bb in range(NB):
                last = nc.vector.tensor_add(ab_f[:, :, bb, :], ab_sum[:, :, :, bb],
                                            pab[:, 0, :, bb].rearrange("p (q r) -> p q r", r=RANK))
            linked(last)
            for ab, (hi, lo) in enumerate(((slice(0, 2), slice(2, 4)), (slice(0, 4, 2), slice(1, 4, 2)))):
                q = slice(2 * ab, 2 * ab + 2)
                st = ab_st[:, q].rearrange("p q b s r -> p (q b) s r")
                full = ab_f[:, q].rearrange("p q b r -> p (q b) r").unsqueeze(2).broadcast_to([P, 2 * NB, 2, RANK])
                linked(nc.vector.tensor_copy(st[:, :, hi, :], full))
                last = nc.vector.tensor_sub(st[:, :, lo, :], full, st[:, :, hi, :])
            last.then_inc(s_abst, 1)
            dve.wait_ge(s_abt, 1)
            nc.vector.tensor_copy(ab_t[:, :, :].rearrange("p q d -> p (q d)"),
                                  p_ab[0:NB * 4 * RANK, :]).then_inc(s_abts, 1)
            dve.wait_ge(s_base, 16)
            for bb in range(NB):
                dve.wait_ge(s_lmm, bb + 1)
                nc.vector.tensor_add(lay_f[:, bb].rearrange("p k n -> p (k n)"),
                                     base_f[:, :, :].rearrange("p k n -> p (k n)"), acc[A][bb][:, :]).then_inc(s_lay, 1)
            for bb in range(NB):
                dve.wait_ge(s_layhi, bb + 1)
                nc.vector.tensor_sub(lay_s[:, 1, bb].rearrange("p k n -> p (k n)"),
                                     lay_f[:, bb].rearrange("p k n -> p (k n)"),
                                     lay_s[:, 0, bb].rearrange("p k n -> p (k n)")).then_inc(s_layer, 1)
            finish_y(1)
            split_y_high(2)
            split_y_low(3)
            linked(nc.vector.tensor_copy(cols(y_cur[:, :, :, :]), cols(y_new[:, :, :, :])))
            dve.sem_clear(s_own)
            vector_half(A, vector_A(False))
            with dve.Fori(0, NBLOCK - 1) as i:
                vector_half(B, vector_B(True))
                vector_half(A, vector_A(True))
            vector_half(B, vector_B(False))
            dve.wait_ge(s_hf[A], 1)
            sum_out(B)
            row_out()


def kernel(x, cond_1024, L0_cond_base_layer, L0_cond_w1, L0_cond_b1, L0_cond_w2, L0_cond_b2, L0_cond_ln_g,
           L0_cond_ln_b, L1_cond_Wx, L1_cond_Wh, L1_cond_b):
    import concourse.bacc as bacc
    from concourse.bass_utils import run_bass_kernel_spmd

    ins = dict(x=x, cond=cond_1024, base=L0_cond_base_layer, w1=L0_cond_w1, b1=L0_cond_b1, w2=L0_cond_w2,
               b2=L0_cond_b2, ln_g=L0_cond_ln_g, ln_b=L0_cond_ln_b, wx=L1_cond_Wx, wh=L1_cond_Wh, b=L1_cond_b)
    nc = bacc.Bacc("TRN2", target_bir_lowering=False, num_devices=1)
    arrays, args = {}, {}
    for name, a in ins.items():
        a = np.ascontiguousarray(a)
        arrays[f"{name}_dram"] = a
        args[name] = nc.dram_tensor(f"{name}_dram", a.shape, mybir.dt.from_np(a.dtype), kind="ExternalInput").ap()
    args["out"] = nc.dram_tensor("out_dram", (NB, T, D), F32, kind="ExternalOutput").ap()
    cond_recurrence(nc, **args)
    r = run_bass_kernel_spmd(nc, [arrays], core_ids=[0])
    return r.results[0]["out_dram"]
```

```python
from contextlib import ExitStack

import numpy as np
import concourse.bass as bass
from concourse import mybir

F32, F16 = mybir.dt.float32, mybir.dt.float16
ACT, ALU = mybir.ActivationFunctionType, mybir.AluOpType

P = 128
NB = 2
T = 1024
D = 256
NM = D // P
RANK = 8
COLS = NM * NB
BLOCK = 32
HALF = BLOCK // 2
NBLOCK = T // BLOCK
PAIRS = HALF // 2
SCALE = 256.0
LN_EPS = 1e-5
A, B = 0, 1


def cond_recurrence(nc, x, cond, base, w1, b1, w2, b2, ln_g, ln_b, wx, wh, b, out):
    ctx = ExitStack()
    with ctx:
        def sb(name, shape, dt=F32):
            return ctx.enter_context(nc.sbuf_tensor(name, shape, dt))

        def pb(name, shape, dt=F32):
            return ctx.enter_context(nc.psum_tensor(name, shape, dt))

        def sem(name):
            return ctx.enter_context(nc.semaphore(name))

        ident = sb("ident", [P, P])
        ident16 = sb("ident16", [P, P], F16)
        wh_f = sb("wh_f", [P, NM, D])
        wx_f = sb("wx_f", [P, NM, D])
        base_f = sb("base_f", [P, NM, D])
        w1_f = sb("w1_f", [P, NM, D])
        w2_f = sb("w2_f", [P, NM, 2 * D * RANK])
        wh_s = sb("wh_s", [P, 2, NM, D], F16)
        wx_s = sb("wx_s", [P, 2, NM, D], F16)
        lay_f = sb("lay_f", [P, NB, NM, D])
        lay_s = sb("lay_s", [P, 2, NB, NM, D], F16)
        b_row = sb("b_row", [1, D])
        b_rest = sb("b_rest", [1, D])
        b_parts = sb("b_parts", [1, 3, D], F16)
        b_w = sb("b_w", [3, D], F16)
        ones = sb("ones", [3, PAIRS * NB], F16)
        cond_r = sb("cond_r", [NB, D])
        cond_n = sb("cond_n", [NB, D])
        cond_c = sb("cond_c", [P, COLS])
        stats = sb("stats", [NB, 6])
        mv = sb("mv", [NB, 2])
        veps = sb("veps", [NB, 1])
        rstd = sb("rstd", [NB, 2])
        warm = sb("warm", [NB, 1])
        vec_r = sb("vec_r", [3 * NM, P])
        vec_c = sb("vec_c", [P, 3, NM])
        ae = sb("ae", [P, NM, NB])
        hid = sb("hid", [P, NM, NB])
        hid_s = sb("hid_s", [P, NM, 2, NB], F16)
        w2_s = sb("w2_s", [P, 2, NM, 2 * D * RANK], F16)
        ab_sum = sb("ab_sum", [P, 4, RANK, NB])
        b2_c = sb("b2_c", [P, 4, RANK])
        ab_f = sb("ab_f", [P, 4, NB, RANK])
        ab_st = sb("ab_st", [P, 4, NB, 4, RANK], F16)
        ab_t = sb("ab_t", [NB * 4 * RANK, 4, P], F16)
        x_in = sb("x_in", [P, P])
        x_f = sb("x_f", [P, BLOCK, NM, NB])
        x_s = sb("x_s", [P, 2, BLOCK, NM, NB], F16)
        y_new = sb("y_new", [P, BLOCK, NM, NB])
        y_cur = sb("y_cur", [P, BLOCK, NM, NB])
        y_s = sb("y_s", [P, 2, BLOCK, NM, NB], F16)
        h_f = sb("h_f", [P, BLOCK, COLS])
        h_hi = sb("h_hi", [P, 2, NM, NB], F16)
        h_lo = sb("h_lo", [P, 2, NM, NB], F16)
        o_sum = sb("o_sum", [P, HALF * COLS])
        o_row = sb("o_row", [HALF * COLS, P])

        acc = [[pb(f"acc{half}{par}", [P, 512]) for par in range(2)] for half in range(2)]
        p_x = pb("p_x", [P, 512])
        p_y = pb("p_y", [P, 512])
        p_o = pb("p_o", [P, 512])
        p_ab = pb("p_ab", [P, 4 * P], F16)

        s_cond, s_vec, s_w1, s_b2, s_base = sem("s_cond"), sem("s_vec"), sem("s_w1"), sem("s_b2"), sem("s_base")
        s_w2 = [sem(f"s_w2_{n}") for n in range(4 * NM)]
        s_wh, s_wx, s_b, s_bw = sem("s_wh"), sem("s_wx"), sem("s_b"), sem("s_bw")
        s_ident = sem("s_ident")
        s_ones = sem("s_ones")
        s_hi = sem("s_hi")
        s_split = sem("s_split")
        s_bparts = sem("s_bparts")
        s_var = sem("s_var")
        s_sqrt = sem("s_sqrt")
        s_norm = sem("s_norm")
        s_turn0 = sem("s_turn0")
        s_condc = sem("s_condc")
        s_vecc = sem("s_vecc")
        s_ae = sem("s_ae")
        s_hmm = sem("s_hmm")
        s_hid = sem("s_hid")
        s_hidhi = sem("s_hidhi")
        s_w2hi = sem("s_w2hi")
        s_w2lo = sem("s_w2lo")
        s_abcol = sem("s_abcol")
        s_abst = sem("s_abst")
        s_abt = sem("s_abt")
        s_abts = sem("s_abts")
        s_lmm = sem("s_lmm")
        s_lay = sem("s_lay")
        s_layhi = sem("s_layhi")
        s_layer = sem("s_layer")
        s_link = sem("s_link")
        s_sum = [sem("s_sumA"), sem("s_sumB")]
        s_hhi = [sem("s_hhiA"), sem("s_hhiB")]
        s_hf = [sem("s_hfA"), sem("s_hfB")]
        s_hlo = [sem("s_hloA"), sem("s_hloB")]
        s_xload = sem("s_xload")
        s_xfree = sem("s_xfree")
        s_xturn = sem("s_xturn")
        s_xsplit = sem("s_xsplit")
        s_ymm = sem("s_ymm")
        s_ysplit = sem("s_ysplit")
        s_osum = sem("s_osum")
        s_oturn = sem("s_oturn")
        s_orow = sem("s_orow")
        s_store = sem("s_store")
        s_ofree = sem("s_ofree")
        s_own = sem("s_own")

        W2_PIECES = [(q, k) for q in range(4) for k in range(NM)]

        def tile_of_ab(q):
            return slice(q * P * RANK, (q + 1) * P * RANK)

        x_rows = x.rearrange("b t (m p) -> t m b p", p=P)
        out_rows = out.rearrange("b t (m p) -> t m b p", p=P)
        cols = lambda ap: ap.rearrange("p t m b -> p (t m b)")

        def take(eng, s, n):
            eng.wait_ge(s, n)
            eng.sem_clear(s)

        PARTS = [(0, 0), (1, 0), (0, 1), (1, 1)]
        LAYER = [(bb, mo, ki, pw, px) for bb in range(NB) for mo in range(NM) for ki in range(NM) for pw, px in PARTS]
        INPUT = [(par, mo, ki, pw, py) for par in range(2)
                 for mo, ki, pw, py in [(mo, None, 0, 0) for mo in range(NM)]
                 + [(mo, ki, pw, py) for mo in range(NM) for ki in range(NM) for pw, py in PARTS]]
        PAUSES = 4

        block = ctx.enter_context(nc.Block())

        @block.sync
        def _(sync):
            sync.dma_start(cond_r[:, :], cond).then_inc(s_cond, 16)
            for n, v in enumerate((ln_g, ln_b, b1)):
                sync.dma_start(vec_r[n * NM:(n + 1) * NM, :], v.rearrange("(m p) -> m p", p=P)).then_inc(s_vec, 16)
            sync.dma_start(w1_f[:, :, :], w1.rearrange("(k p) n -> p k n", p=P)).then_inc(s_w1, 16)
            for n, (q, k) in enumerate(W2_PIECES):
                sync.dma_start(w2_f[:, k, tile_of_ab(q)], w2[k * P:(k + 1) * P, tile_of_ab(q)]).then_inc(s_w2[n], 16)
            sync.dma_start(base_f[:, :, :], base.rearrange("(k p) n -> p k n", p=P)).then_inc(s_base, 16)
            sync.dma_start(x_in[:, :], x_rows[0:BLOCK]).then_inc(s_xload, 16)
            sync.dma_start(wh_f[:, :, :], wh.rearrange("(k p) n -> p k n", p=P)).then_inc(s_wh, 16)
            sync.dma_start(wx_f[:, :, :], wx.rearrange("(k p) n -> p k n", p=P)).then_inc(s_wx, 16)
            sync.wait_ge(s_xfree, 1)
            sync.dma_start(x_in[:, :], x_rows[BLOCK:2 * BLOCK]).then_inc(s_xload, 16)
            sync.sem_inc(s_ofree, 1)

            def store(q, t0, more=True):
                sync.wait_ge(s_orow, q + 1)
                sync.dma_start(out_rows[t0], o_row[:, :]).then_inc(s_store, 16)
                sync.wait_ge(s_store, (q + 1) * 16)
                if more:
                    sync.sem_inc(s_ofree, 1)

            with sync.Fori(0, NBLOCK - 2) as i:
                sync.wait_ge(s_xfree, i + 2)
                sync.dma_start(x_in[:, :], x_rows[bass.ds((i + 2) * BLOCK, BLOCK)]).then_inc(s_xload, 16)
                for half in range(2):
                    store(i * 2 + half, bass.ds(i * BLOCK + half * HALF, HALF))
            for q in range(2 * (NBLOCK - 2), 2 * NBLOCK):
                store(q, slice(q * HALF, (q + 1) * HALF), more=q < 2 * NBLOCK - 1)

        @block.gpsimd
        def _(pool):
            nc.gpsimd.memset(ident[:, :], 0.0).then_inc(s_ident, 1)
            nc.gpsimd.memset(ident16[:, :], 0.0).then_inc(s_ident, 1)
            nc.gpsimd.memset(ones[:, :], 1.0).then_inc(s_ones, 1)
            pool.wait_ge(s_ident, 2)
            for e in (ident, ident16):
                nc.gpsimd.affine_select(out=e[:, :], in_=e[:, :], compare_op=ALU.not_equal, fill=1.0,
                                        base=0, pattern=[[-1, P]], channel_multiplier=1).then_inc(s_ident, 1)
            pool.dma_start(b_row[:, :], b.rearrange("(a n) -> a n", a=1)).then_inc(s_b, 16)
            pool.dma_start(b2_c[:, :, :], b2.rearrange("(q p r) -> p q r", q=4, r=RANK)).then_inc(s_b2, 16)
            def step(n, ins):
                ins.then_inc(s_bparts, 1)
                pool.wait_ge(s_bparts, n)
            pool.wait_ge(s_b, 16)
            step(1, nc.gpsimd.tensor_scalar(b_row[:, :], b_row[:, :], SCALE, None, ALU.mult))
            step(2, nc.gpsimd.tensor_copy(b_parts[:, 0, :], b_row[:, :]))
            step(3, nc.gpsimd.tensor_sub(b_rest[:, :], b_row[:, :], b_parts[:, 0, :]))
            step(4, nc.gpsimd.tensor_copy(b_parts[:, 1, :], b_rest[:, :]))
            step(5, nc.gpsimd.tensor_sub(b_parts[:, 2, :], b_rest[:, :], b_parts[:, 1, :]))
            pool.dma_start(b_w[:, :], b_parts[0:1, :, :]).then_inc(s_bw, 16)

        @block.tensor
        def _(pe):
            def turn_x():
                take(pe, s_xload, 16)
                nc.tensor.transpose(p_x[:, 0:P], x_in[:, :], ident[:, :]).then_inc(s_xturn, 1)

            def turn_out():
                take(pe, s_osum, 1)
                nc.tensor.transpose(p_o[0:HALF * COLS, 0:P], o_sum[:, :], ident[:, :]).then_inc(s_oturn, 1)

            def layer_products(todo):
                py = p_y[:, 0:P].rearrange("p (t m b) -> p t m b", m=NM, b=NB)
                for bb, mo, ki, pw, px in todo:
                    last = nc.tensor.matmul(py[:, :, mo, bb], lay_s[:, pw, bb, ki, mo * P:(mo + 1) * P],
                                            x_s[:, px, :, ki, bb], start=(bb, mo, ki, pw, px) == LAYER[0],
                                            stop=True, skip_group_check=True)
                return last

            def input_products(half, todo):
                for par, mo, ki, pw, py in todo:
                    dst = acc[half][par][:, 0:PAIRS * COLS].rearrange("p (t m b) -> p t m b", m=NM, b=NB)[:, :, mo, :]
                    out_channels = slice(mo * P, (mo + 1) * P)
                    if ki is None:
                        nc.tensor.matmul(dst, b_w[:, out_channels], ones[:, :], start=mo == 0, stop=True,
                                         skip_group_check=True)
                    else:
                        t0 = half * HALF + par
                        nc.tensor.matmul(dst, wx_s[:, pw, ki, out_channels], y_s[:, py, t0:t0 + HALF - 1:2, ki, :],
                                         start=False, stop=True, skip_group_check=True)

            def share(todo, k):
                n = len(todo) // PAUSES
                return todo[k * n:(k + 1) * n]

            def chain_step(half, u):
                par = u % 2
                dst = acc[half][par][:, (u // 2) * COLS:(u // 2 + 1) * COLS]
                pe.wait_ge(s_hhi[half], u + 1)
                for pw in range(2):
                    for mo in range(NM):
                        for ki in range(NM):
                            nc.tensor.matmul(dst[:, mo * NB:(mo + 1) * NB], wh_s[:, pw, ki, mo * P:(mo + 1) * P],
                                             h_hi[:, par, ki, :], start=False, stop=True, skip_group_check=True)
                pe.wait_ge(s_hlo[half], u + 1)
                for mo in range(NM):
                    for ki in range(NM):
                        last = nc.tensor.matmul(dst[:, mo * NB:(mo + 1) * NB], wh_s[:, 0, ki, mo * P:(mo + 1) * P],
                                                h_lo[:, par, ki, :], start=False, stop=True, skip_group_check=True)
                last.then_inc(s_sum[half], 1)

            def half_a(first=False):
                for u in range(HALF):
                    chain_step(A, u)
                    if first and u == 0:
                        input_products(A, INPUT[len(INPUT) // 2:])
                    if not first and u == 1:
                        turn_out()
                    if 2 <= u < 2 + PAUSES:
                        input_products(B, share(INPUT, u - 2))
                pe.sem_clear(s_hhi[A])
                pe.sem_clear(s_hlo[A])

            def half_b(last=False):
                for u in range(HALF):
                    chain_step(B, u)
                    if u == 1:
                        turn_out()
                    if last:
                        continue
                    if u == 0:
                        turn_x()
                    if u == 4:
                        take(pe, s_xsplit, 1)
                    if 4 <= u < 4 + PAUSES:
                        product = layer_products(share(LAYER, u - 4))
                    if u == 3 + PAUSES:
                        product.then_inc(s_ymm, 1)
                    if u == HALF - PAUSES:
                        take(pe, s_ysplit, 1)
                    if u >= HALF - PAUSES:
                        input_products(A, share(INPUT, u - (HALF - PAUSES)))
                pe.sem_clear(s_hhi[B])
                pe.sem_clear(s_hlo[B])

            pe.wait_ge(s_ident, 4)
            pe.wait_ge(s_cond, 16)
            for k in range(NM):
                nc.tensor.transpose(p_x[:, k * NB:(k + 1) * NB], cond_r[:, k * P:(k + 1) * P], ident[0:NB, 0:NB])
            pe.wait_ge(s_vec, 48)
            nc.tensor.transpose(p_x[:, 64:64 + 3 * NM], vec_r[:, :], ident[0:3 * NM, 0:3 * NM]).then_inc(s_turn0, 1)
            pe.wait_ge(s_norm, 1)
            for k in range(NM):
                last = nc.tensor.transpose(p_y[:, k * NB:(k + 1) * NB], cond_n[:, k * P:(k + 1) * P],
                                           ident[0:NB, 0:NB])
            last.then_inc(s_turn0, 1)
            pe.wait_ge(s_ae, 1)
            pe.wait_ge(s_w1, 16)
            for mo in range(NM):
                for k in range(NM):
                    last = nc.tensor.matmul(p_o[:, mo * NB:(mo + 1) * NB], w1_f[:, k, mo * P:(mo + 1) * P],
                                            ae[:, k, :], start=k == 0, stop=k == NM - 1)
            last.then_inc(s_hmm, 1)
            pe.wait_ge(s_hid, 1)
            for n, (q, k) in enumerate(W2_PIECES):
                if n == 6:
                    turn_x()
                for pw, ready in ((0, s_w2hi), (1, s_w2lo)):
                    pe.wait_ge(ready, n + 1)
                    for r in range(RANK):
                        c = 64 + (q * RANK + r) * 2 * NB
                        w = w2_s[:, pw, k, tile_of_ab(q)].rearrange("p (d r) -> p r d", r=RANK)
                        last = nc.tensor.matmul(p_y[:, c:c + 2 * NB], w[:, r, :],
                                                hid_s[:, k].rearrange("p s b -> p (s b)"),
                                                start=n == 0 and pw == 0 and r == 0, stop=True, skip_group_check=True)
            last.then_inc(s_abcol, 1)
            pe.wait_ge(s_abst, 1)
            for q in range(4):
                last = nc.tensor.transpose(p_ab[0:NB * 4 * RANK, q * P:(q + 1) * P],
                                           ab_st[:, q].rearrange("p b s r -> p (b s r)"), ident16[:, :])
            last.then_inc(s_abt, 1)
            pe.wait_ge(s_abts, 1)
            for bb in range(NB):
                rows = slice(bb * 4 * RANK, (bb + 1) * 4 * RANK)
                for k in range(NM):
                    last = nc.tensor.matmul(acc[A][bb][:, k * D:(k + 1) * D], ab_t[rows, k, :],
                                            ab_t[rows, 2:4, :].rearrange("p k d -> p (k d)"), start=k == 0, stop=True,
                                            skip_group_check=True)
                last.then_inc(s_lmm, 1)
            take(pe, s_xsplit, 1)
            for bb in range(NB):
                pe.wait_ge(s_layer, bb + 1)
                product = layer_products([p for p in LAYER if p[0] == bb])
            product.then_inc(s_ymm, 1)
            take(pe, s_ysplit, 1)
            pe.wait_ge(s_split, 2)
            pe.wait_ge(s_bw, 16)
            pe.wait_ge(s_ones, 1)
            input_products(A, INPUT[:len(INPUT) // 2])
            half_a(first=True)
            with pe.Fori(0, NBLOCK - 1):
                half_b()
                half_a()
            half_b(last=True)
            turn_out()

        @block.scalar
        def _(act):
            def give_h(n, src, func, scale, last=False):
                half, par, slot = (n // HALF) % 2, n % 2, (n - 1) % BLOCK
                if not last:
                    nc.scalar.activation(h_hi[:, par].rearrange("p m b -> p (m b)"), src, func,
                                         scale=scale).then_inc(s_hhi[half], 1)
                nc.scalar.activation(h_f[:, slot, :], src, func, scale=scale).then_inc(s_hf[half], 1)

            def half_block(half, last=False):
                for u in range(HALF):
                    act.wait_ge(s_sum[half], u + 1)
                    give_h(half * HALF + u + 1, acc[half][u % 2][:, (u // 2) * COLS:(u // 2 + 1) * COLS],
                           ACT.Tanh, 1.0 / SCALE, last=last and u == HALF - 1)
                act.sem_clear(s_sum[half])

            act.wait_ge(s_var, 1)
            nc.scalar.activation(rstd[:, 1:2], veps[:, :], ACT.Sqrt).then_inc(s_sqrt, 1)
            nc.scalar.activation(warm[:, :], veps[:, :], ACT.Gelu)
            act.wait_ge(s_hmm, 1)
            act.wait_ge(s_vecc, 1)
            for m in range(NM):
                for dst in (hid_s[:, m, 0, :], hid[:, m, :]):
                    last = nc.scalar.activation(dst, p_o[:, m * NB:(m + 1) * NB], ACT.Gelu, bias=vec_c[:, 2, m:m + 1])
            last.then_inc(s_hidhi, 1)

            def high(dst, src, s):
                act.wait_ge(s, 16)
                nc.scalar.activation(dst[:, 0].rearrange("p k n -> p (k n)"),
                                     src[:, :, :].rearrange("p k n -> p (k n)"), ACT.Copy,
                                     scale=SCALE).then_inc(s_hi, 1)

            for n, (q, k) in enumerate(W2_PIECES):
                act.wait_ge(s_w2[n], 16)
                nc.scalar.copy(w2_s[:, 0, k, tile_of_ab(q)], w2_f[:, k, tile_of_ab(q)]).then_inc(s_w2hi, 1)
            high(wh_s, wh_f, s_wh)
            high(wx_s, wx_f, s_wx)
            for bb in range(NB):
                act.wait_ge(s_lay, bb + 1)
                nc.scalar.copy(lay_s[:, 0, bb].rearrange("p k n -> p (k n)"),
                               lay_f[:, bb].rearrange("p k n -> p (k n)")).then_inc(s_layhi, 1)
            act.wait_ge(s_condc, 1)
            give_h(0, cond_c[:, :], ACT.Copy, 1.0)
            half_block(A)
            with act.Fori(0, NBLOCK - 1):
                half_block(B)
                half_block(A)
            half_block(B, last=True)

        @block.vector
        def _(dve):
            def split_x_high():
                take(dve, s_xturn, 1)
                nc.vector.tensor_copy(cols(x_f[:, :, :, :]), p_x[:, 0:P]).then_inc(s_xfree, 1)
                nc.vector.tensor_copy(cols(x_s[:, 0]), p_x[:, 0:P]).then_inc(s_own, 1)

            def split_x_low():
                dve.wait_ge(s_own, 1)
                nc.vector.tensor_sub(cols(x_s[:, 1]), p_x[:, 0:P], cols(x_s[:, 0])).then_inc(s_xsplit, 1)

            def finish_y():
                take(dve, s_ymm, 1)
                nc.vector.scalar_tensor_tensor(cols(y_new[:, :, :, :]), cols(x_f[:, :, :, :]), 2.0, p_y[:, 0:P],
                                               ALU.mult, ALU.add).then_inc(s_own, 1)

            def split_y_high():
                dve.wait_ge(s_own, 2)
                nc.vector.tensor_copy(cols(y_s[:, 0]), cols(y_new[:, :, :, :])).then_inc(s_own, 1)

            def split_y_low():
                take(dve, s_own, 3)
                nc.vector.tensor_sub(cols(y_s[:, 1]), cols(y_new[:, :, :, :]), cols(y_s[:, 0])).then_inc(s_ysplit, 1)

            def keep_y():
                nc.vector.tensor_copy(cols(y_cur[:, :, :, :]), cols(y_new[:, :, :, :])).then_inc(s_own, 1)
                take(dve, s_own, 1)

            def sum_out(half):
                steps = slice(half * HALF, (half + 1) * HALF)
                nc.vector.tensor_add(o_sum[:, :], cols(y_cur[:, steps]),
                                     h_f[:, steps, :].rearrange("p t c -> p (t c)")).then_inc(s_osum, 1)

            def row_out():
                take(dve, s_oturn, 1)
                take(dve, s_ofree, 1)
                nc.vector.tensor_copy(o_row[:, :], p_o[0:HALF * COLS, 0:P]).then_inc(s_orow, 1)

            def chain_step(half, u):
                par, slot = u % 2, (half * HALF + u - 1) % BLOCK
                dve.wait_ge(s_hf[half], u + 1)
                nc.vector.tensor_sub(h_lo[:, par].rearrange("p m b -> p (m b)"), h_f[:, slot, :],
                                     h_hi[:, par].rearrange("p m b -> p (m b)")).then_inc(s_hlo[half], 1)

            def half_a(first=False):
                for u in range(HALF):
                    chain_step(A, u)
                    if first:
                        continue
                    if u == 0:
                        sum_out(B)
                    if u == 2:
                        keep_y()
                    if u == 3:
                        row_out()
                dve.sem_clear(s_hf[A])

            def half_b(last=False):
                for u in range(HALF):
                    chain_step(B, u)
                    if u == 0:
                        sum_out(A)
                    if u == 3:
                        row_out()
                    if last:
                        continue
                    if u == 1:
                        split_x_high()
                    if u == 2:
                        split_x_low()
                    if u == 8:
                        finish_y()
                    if u == 9:
                        split_y_high()
                    if u == 10:
                        split_y_low()
                dve.sem_clear(s_hf[B])

            count = [0]

            def linked(ins):
                count[0] += 1
                ins.then_inc(s_link, 1)
                dve.wait_ge(s_link, count[0])

            dve.wait_ge(s_cond, 16)
            linked(nc.vector.bn_stats(stats[:, :], cond_r[:, :]))
            linked(nc.vector.bn_aggr(mv[:, :], stats[:, :]))
            linked(nc.vector.tensor_scalar(veps[:, :], mv[:, 1:2], LN_EPS, None, ALU.add))
            dve.sem_inc(s_var, 1)
            dve.wait_ge(s_sqrt, 1)
            linked(nc.vector.reciprocal(rstd[:, 0:1], rstd[:, 1:2]))
            linked(nc.vector.tensor_scalar(rstd[:, 1:2], rstd[:, 0:1], rstd[:, 0:1], veps[:, 0:1], ALU.mult, ALU.mult))
            linked(nc.vector.tensor_scalar(rstd[:, 1:2], rstd[:, 1:2], -0.5, 1.5, ALU.mult, ALU.add))
            linked(nc.vector.tensor_mul(rstd[:, 0:1], rstd[:, 0:1], rstd[:, 1:2]))
            nc.vector.tensor_scalar(cond_n[:, :], cond_r[:, :], mv[:, 0:1], rstd[:, 0:1],
                                    ALU.subtract, ALU.mult).then_inc(s_norm, 1)
            dve.wait_ge(s_turn0, 1)
            nc.vector.tensor_copy(cond_c[:, :], p_x[:, 0:COLS]).then_inc(s_condc, 1)
            nc.vector.tensor_copy(vec_c[:, :, :].rearrange("p v m -> p (v m)"),
                                  p_x[:, 64:64 + 3 * NM]).then_inc(s_vecc, 1)
            dve.wait_ge(s_vecc, 1)
            dve.wait_ge(s_turn0, 2)
            for k in range(NM):
                last = nc.vector.tensor_scalar(ae[:, k, :], p_y[:, k * NB:(k + 1) * NB], vec_c[:, 0, k:k + 1],
                                               vec_c[:, 1, k:k + 1], ALU.mult, ALU.add)
            last.then_inc(s_ae, 1)
            dve.wait_ge(s_hidhi, 1)
            nc.vector.tensor_sub(hid_s[:, :, 1, :], hid[:, :, :], hid_s[:, :, 0, :]).then_inc(s_hid, 1)

            def low(dst, src, n):
                dve.wait_ge(s_hi, n + 1)
                nc.vector.scalar_tensor_tensor(
                    dst[:, 1].rearrange("p k n -> p (k n)"), src[:, :, :].rearrange("p k n -> p (k n)"), SCALE,
                    dst[:, 0].rearrange("p k n -> p (k n)"), ALU.mult, ALU.subtract).then_inc(s_split, 1)

            for n, (q, k) in enumerate(W2_PIECES):
                dve.wait_ge(s_w2hi, n + 1)
                nc.vector.tensor_sub(w2_s[:, 1, k, tile_of_ab(q)], w2_f[:, k, tile_of_ab(q)],
                                     w2_s[:, 0, k, tile_of_ab(q)]).then_inc(s_w2lo, 1)
            split_x_high()
            split_x_low()
            dve.wait_ge(s_b2, 16)
            dve.wait_ge(s_abcol, 1)
            pab = p_y[:, 64:64 + 4 * RANK * 2 * NB].rearrange("p (c s b) -> p s c b", s=2, b=NB)
            linked(nc.vector.tensor_add(ab_sum[:, :, :, :].rearrange("p q r b -> p (q r) b"), pab[:, 1],
                                        b2_c[:, :, :].rearrange("p q r -> p (q r)").unsqueeze(2)
                                        .broadcast_to([P, 4 * RANK, NB])))
            for bb in range(NB):
                last = nc.vector.tensor_add(ab_f[:, :, bb, :], ab_sum[:, :, :, bb],
                                            pab[:, 0, :, bb].rearrange("p (q r) -> p q r", r=RANK))
            linked(last)
            for ab, (hi, lo) in enumerate(((slice(0, 2), slice(2, 4)), (slice(0, 4, 2), slice(1, 4, 2)))):
                q = slice(2 * ab, 2 * ab + 2)
                st = ab_st[:, q].rearrange("p q b s r -> p (q b) s r")
                full = ab_f[:, q].rearrange("p q b r -> p (q b) r").unsqueeze(2).broadcast_to([P, 2 * NB, 2, RANK])
                linked(nc.vector.tensor_copy(st[:, :, hi, :], full))
                last = nc.vector.tensor_sub(st[:, :, lo, :], full, st[:, :, hi, :])
            last.then_inc(s_abst, 1)
            low(wh_s, wh_f, 0)
            dve.wait_ge(s_abt, 1)
            nc.vector.tensor_copy(ab_t[:, :, :].rearrange("p q d -> p (q d)"),
                                  p_ab[0:NB * 4 * RANK, :]).then_inc(s_abts, 1)
            low(wx_s, wx_f, 1)
            dve.wait_ge(s_base, 16)
            for bb in range(NB):
                dve.wait_ge(s_lmm, bb + 1)
                nc.vector.tensor_add(lay_f[:, bb].rearrange("p k n -> p (k n)"),
                                     base_f[:, :, :].rearrange("p k n -> p (k n)"), acc[A][bb][:, :]).then_inc(s_lay, 1)
            for bb in range(NB):
                dve.wait_ge(s_layhi, bb + 1)
                nc.vector.tensor_sub(lay_s[:, 1, bb].rearrange("p k n -> p (k n)"),
                                     lay_f[:, bb].rearrange("p k n -> p (k n)"),
                                     lay_s[:, 0, bb].rearrange("p k n -> p (k n)")).then_inc(s_layer, 1)
            finish_y()
            split_y_high()
            split_y_low()
            keep_y()
            half_a(first=True)
            with dve.Fori(0, NBLOCK - 1):
                half_b()
                half_a()
            half_b(last=True)
            dve.wait_ge(s_hf[A], 1)
            sum_out(B)
            row_out()


def kernel(x, cond_1024, L0_cond_base_layer, L0_cond_w1, L0_cond_b1, L0_cond_w2, L0_cond_b2, L0_cond_ln_g,
           L0_cond_ln_b, L1_cond_Wx, L1_cond_Wh, L1_cond_b):
    import concourse.bacc as bacc
    from concourse.bass_utils import run_bass_kernel_spmd

    ins = dict(x=x, cond=cond_1024, base=L0_cond_base_layer, w1=L0_cond_w1, b1=L0_cond_b1, w2=L0_cond_w2,
               b2=L0_cond_b2, ln_g=L0_cond_ln_g, ln_b=L0_cond_ln_b, wx=L1_cond_Wx, wh=L1_cond_Wh, b=L1_cond_b)
    nc = bacc.Bacc("TRN2", target_bir_lowering=False, num_devices=1)
    arrays, args = {}, {}
    for name, a in ins.items():
        a = np.ascontiguousarray(a)
        arrays[f"{name}_dram"] = a
        args[name] = nc.dram_tensor(f"{name}_dram", a.shape, mybir.dt.from_np(a.dtype), kind="ExternalInput").ap()
    args["out"] = nc.dram_tensor("out_dram", (NB, T, D), F32, kind="ExternalOutput").ap()
    cond_recurrence(nc, **args)
    r = run_bass_kernel_spmd(nc, [arrays], core_ids=[0])
    return r.results[0]["out_dram"]
```
